# Optimizing a Trainium2 kernel written in Bass

```python
import numpy as np
import jax
import jax.numpy as jnp

def _softmax(x, axis=-1):
    return jax.nn.softmax(x, axis=axis)

def _gelu(x):
    return jax.nn.gelu(x, approximate=True)

def _silu(x):
    return jax.nn.silu(x)

def _sigmoid(x):
    return jax.nn.sigmoid(x)

def _layernorm(x, axis=-1, eps=1e-05):
    m = jnp.mean(x, axis=axis, keepdims=True)
    v = jnp.var(x, axis=axis, keepdims=True)
    return (x - m) / jnp.sqrt(v + eps)

def _scatter_add(tgt, idx, src, axis=0):
    return tgt.at[idx].add(src)

def _segment_sum(src, seg, n):
    return jax.ops.segment_sum(src, seg, n)
kernel_name = 'mk_adj_preln_d4_adj_r2_bf2382'

def setup_inputs(seed: int=0):
    np.random.seed(seed)
    _w = jnp.asarray

    def _rec_inputs():
        import jax
        import jax.numpy as jnp
        _gk = jax.random.key(seed)
        x = -0.0003929 + 0.9999 * jax.random.normal(jax.random.fold_in(_gk, 1), (128, 128, 256), jnp.float32)
        _a = jax.random.bernoulli(jax.random.fold_in(_gk, 2), 0.03125, (128, 128, 128))
        _a = jnp.logical_or(_a, jnp.eye(128, dtype=bool))
        _af = _a.astype(jnp.float32)
        _af = _af * jax.random.uniform(jax.random.fold_in(_gk, 3), (128, 128, 128), jnp.float32, 0.05, 1)
        adj = _af
        return (x, adj)
    x, adj = _rec_inputs()

    def _L0_gnn_setup():
        import jax, jax.numpy as jnp
        import numpy as np
        EPS = 1e-06
        key = jax.random.key(seed)
        k1, k2, k3 = jax.random.split(key, 3)
        B, N, F, O = (8, 2048, 256, 256)
        x = jax.random.normal(k1, (B, N, F), dtype=jnp.float32)
        adj = jax.random.uniform(k2, (B, N, N), dtype=jnp.float32)
        W = jax.random.normal(k3, (O, 2 * F), dtype=jnp.float32) * (1.0 / np.sqrt(2 * F))
        return {'x': x, 'adj': adj, 'W': W}
    _L0_gnn_all = _L0_gnn_setup()
    _L0_gnn_in = {k: v for k, v in _L0_gnn_all.items() if k in ('W',)}
    del _L0_gnn_all

    def _L1_gnn_setup():
        import jax, jax.numpy as jnp
        import numpy as np
        IN_DIM = 256
        ATT_DIM = 64
        B, N = (4, 2048)
        key = jax.random.key(seed)
        k1, k2, k3, k4 = jax.random.split(key, 4)
        x = jax.random.normal(k1, (B, N, IN_DIM), dtype=jnp.float32)
        adj_matrix = (jax.random.uniform(k2, (B, N, N)) < 0.05).astype(jnp.float32)
        W_qk = jax.random.normal(k3, (2 * ATT_DIM, IN_DIM), dtype=jnp.float32) / np.sqrt(IN_DIM)
        W_v = jax.random.normal(k4, (IN_DIM, IN_DIM), dtype=jnp.float32) / np.sqrt(IN_DIM)
        return {'x': x, 'adj_matrix': adj_matrix, 'W_qk': W_qk, 'W_v': W_v}
    _L1_gnn_all = _L1_gnn_setup()
    _L1_gnn_in = {k: v for k, v in _L1_gnn_all.items() if k in ('W_qk', 'W_v')}
    del _L1_gnn_all

    def _L2_gnn_setup():
        import jax, jax.numpy as jnp
        import numpy as np
        B, N, F_IN, F_HID, F_OUT = (32, 512, 256, 256, 256)

        def _gcn_layer(x, adj, W, b):
            support = jnp.einsum('bnf,fh->bnh', x, W)
            return jnp.einsum('bnm,bmh->bnh', adj, support) + b
        key = jax.random.key(seed)
        ks = jax.random.split(key, 8)

        def xavier(k, fan_in, fan_out):
            bound = float(np.sqrt(6.0 / (fan_in + fan_out)))
            return jax.random.uniform(k, (fan_in, fan_out), jnp.float32, -bound, bound)
        return {'batch_graph': jax.random.normal(ks[0], (B, N, F_IN), jnp.float32), 'adj': jax.random.uniform(ks[1], (B, N, N), jnp.float32), 'W1': xavier(ks[2], F_IN, F_HID), 'b1': jnp.zeros((F_HID,), jnp.float32), 'W2': xavier(ks[3], F_HID, F_HID), 'b2': jnp.zeros((F_HID,), jnp.float32), 'W3': xavier(ks[4], F_HID, F_OUT), 'b3': jnp.zeros((F_OUT,), jnp.float32)}
    _L2_gnn_all = _L2_gnn_setup()
    _L2_gnn_in = {k: v for k, v in _L2_gnn_all.items() if k in ('W1', 'b1', 'W2', 'b2', 'W3', 'b3')}
    del _L2_gnn_all

    def _L3_gnn_setup():
        import jax, jax.numpy as jnp
        import numpy as np
        B, N, DIN, DOUT, K = (4, 1024, 256, 256, 3)
        key = jax.random.key(seed)
        ks = jax.random.split(key, 8)
        X = jax.random.normal(ks[0], (B, N, DIN), dtype=jnp.float32)
        A = jax.random.uniform(ks[1], (B, N, N), dtype=jnp.float32)
        Wv = jax.random.normal(ks[2], (DIN, DOUT), dtype=jnp.float32) * 0.02
        bv = jax.random.normal(ks[3], (DOUT,), dtype=jnp.float32) * 0.02
        aw = jax.random.normal(ks[4], (2 * DOUT, 1), dtype=jnp.float32) * 0.05
        ab = jax.random.normal(ks[5], (1,), dtype=jnp.float32) * 0.05
        Wk = jax.random.normal(ks[6], (K, DIN, DOUT), dtype=jnp.float32) * 0.02
        bk = jax.random.normal(ks[7], (K, DOUT), dtype=jnp.float32) * 0.02
        return {'X': X, 'A': A, 'Wv': Wv, 'bv': bv, 'aw': aw, 'ab': ab, 'Wk': Wk, 'bk': bk}
    _L3_gnn_all = _L3_gnn_setup()
    _L3_gnn_in = {k: v for k, v in _L3_gnn_all.items() if k in ('Wv', 'bv', 'aw', 'ab', 'Wk', 'bk')}
    del _L3_gnn_all
    return {'x': x, 'adj': adj, 'L0_gnn_W': _L0_gnn_in['W'], 'L1_gnn_W_qk': _L1_gnn_in['W_qk'], 'L1_gnn_W_v': _L1_gnn_in['W_v'], 'L2_gnn_W1': _L2_gnn_in['W1'], 'L2_gnn_b1': _L2_gnn_in['b1'], 'L2_gnn_W2': _L2_gnn_in['W2'], 'L2_gnn_b2': _L2_gnn_in['b2'], 'L2_gnn_W3': _L2_gnn_in['W3'], 'L2_gnn_b3': _L2_gnn_in['b3'], 'L3_gnn_Wv': _L3_gnn_in['Wv'], 'L3_gnn_bv': _L3_gnn_in['bv'], 'L3_gnn_aw': _L3_gnn_in['aw'], 'L3_gnn_ab': _L3_gnn_in['ab'], 'L3_gnn_Wk': _L3_gnn_in['Wk'], 'L3_gnn_bk': _L3_gnn_in['bk']}

def reference(x, adj, L0_gnn_W, L1_gnn_W_qk, L1_gnn_W_v, L2_gnn_W1, L2_gnn_b1, L2_gnn_W2, L2_gnn_b2, L2_gnn_W3, L2_gnn_b3, L3_gnn_Wv, L3_gnn_bv, L3_gnn_aw, L3_gnn_ab, L3_gnn_Wk, L3_gnn_bk):
    import jax
    import jax.numpy as jnp

    def _L0_gnn_ref(x, adj, W):
        import jax, jax.numpy as jnp
        import numpy as np
        EPS = 1e-06
        deg = jnp.sum(adj, axis=-1, keepdims=True)
        agg = jnp.einsum('bij,bjf->bif', adj, x) / jnp.maximum(deg, EPS)
        cat = jnp.concatenate([x, agg], axis=2)
        out = jnp.einsum('bnf,of->bno', cat, W)
        return jax.nn.relu(out)

    def _L1_gnn_ref(x, adj_matrix, W_qk, W_v):
        import jax, jax.numpy as jnp
        import numpy as np
        IN_DIM = 256
        ATT_DIM = 64
        B, N = (4, 2048)
        qk = jnp.einsum('bnd,ed->bne', x, W_qk)
        q, k = jnp.split(qk, 2, axis=-1)
        v = jnp.einsum('bnd,ed->bne', x, W_v)
        inv_scale = 1.0 / ATT_DIM ** 0.5
        scores = jnp.einsum('bnd,bmd->bnm', q, k) * inv_scale
        w = jnp.sum(scores * adj_matrix, axis=-1, keepdims=True)
        w = jax.nn.softmax(w, axis=1)
        return w * v

    def _L2_gnn_ref(batch_graph, adj, W1, b1, W2, b2, W3, b3):
        import jax, jax.numpy as jnp
        import numpy as np
        B, N, F_IN, F_HID, F_OUT = (32, 512, 256, 256, 256)

        def _gcn_layer(x, adj, W, b):
            support = jnp.einsum('bnf,fh->bnh', x, W)
            return jnp.einsum('bnm,bmh->bnh', adj, support) + b
        x = jax.nn.relu(_gcn_layer(batch_graph, adj, W1, b1))
        x = jax.nn.relu(_gcn_layer(x, adj, W2, b2))
        out = _gcn_layer(x, adj, W3, b3)
        return out

    def _L3_gnn_ref(X, A, Wv, bv, aw, ab, Wk, bk):
        import jax, jax.numpy as jnp
        import numpy as np
        B, N, DIN, DOUT, K = (4, 1024, 256, 256, 3)
        d = Wv.shape[1]
        Xw = X @ Wv + bv
        sj = Xw @ aw[:d, 0]
        si = Xw @ aw[d:, 0]
        e = jax.nn.leaky_relu(sj[:, None, :] + si[:, :, None] + ab[0], negative_slope=0.2)
        alpha_matrix = A * jnp.exp(e)
        transition = alpha_matrix / (jnp.sum(alpha_matrix, axis=-1, keepdims=True) + 1e-12)
        H = jnp.zeros(X.shape[:-1] + (d,), dtype=X.dtype)
        Xk = X
        for k in range(Wk.shape[0]):
            H = H + Xk @ Wk[k] + bk[k]
            Xk = jnp.einsum('bij,bjd->bid', transition, Xk)
        return jax.nn.relu(H)
    h = jnp.maximum(_layernorm(x, axis=-1), 0.0)
    x = x + _L0_gnn_ref(h, adj, L0_gnn_W)
    h = jnp.maximum(_layernorm(x, axis=-1), 0.0)
    x = x + _L1_gnn_ref(h, adj, L1_gnn_W_qk, L1_gnn_W_v)
    h = jnp.maximum(_layernorm(x, axis=-1), 0.0)
    x = x + _L2_gnn_ref(h, adj, L2_gnn_W1, L2_gnn_b1, L2_gnn_W2, L2_gnn_b2, L2_gnn_W3, L2_gnn_b3)
    h = jnp.maximum(_layernorm(x, axis=-1), 0.0)
    x = x + _L3_gnn_ref(h, adj, L3_gnn_Wv, L3_gnn_bv, L3_gnn_aw, L3_gnn_ab, L3_gnn_Wk, L3_gnn_bk)
    return x

_drawn_inputs = setup_inputs


def setup_inputs(seed=0):
    import zlib

    import numpy as np

    out = dict(_drawn_inputs(seed))
    spreads = {'L2_gnn_b1': (0.0, 0.1), 'L2_gnn_b2': (0.0, 0.1), 'L2_gnn_b3': (0.0, 0.354)}
    factors = {'L1_gnn_W_qk': 8.0,
     'L1_gnn_W_v': 8.0,
     'L3_gnn_Wv': 8.0,
     'L3_gnn_bv': 8.0,
     'L3_gnn_aw': 8.0,
     'L3_gnn_bk': 8.0}
    for name, (base, spread) in spreads.items():
        noise = np.random.default_rng([zlib.crc32(name.encode()), seed]).standard_normal(out[name].shape)
        drawn = base * np.exp(spread * noise) if base else spread * noise
        out[name] = jnp.asarray(drawn.astype(out[name].dtype))
    for name, factor in factors.items():
        out[name] = (out[name] * factor).astype(out[name].dtype)
    return out
```

```python
from contextlib import ExitStack

import concourse.bass as bass
from concourse import mybir

F32 = mybir.dt.float32
F32R = mybir.dt.float32r
ALU = mybir.AluOpType
ACT = mybir.ActivationFunctionType
AX_X = mybir.AxisListType.X

P = 128
BANKS = 8
LAYERNORM_EPS = 1e-5
DEGREE_EPS = 1e-6
ROW_SUM_EPS = 1e-12
LEAKY_SLOPE = 0.2
SMALL_LOADS = 7

PHASE_LAG = {"A": 0, "B": 1, "C": 2}
PLACES = [
    ("A", "norm0", 0.0), ("A", "adj_norm", 1.0), ("A", "turn0", 4.0), ("A", "sage_y", 7.0), ("A", "sage", 10.0),
    ("A", "norm1", 12.0), ("A", "turn1", 17.0), ("A", "qk", 20.0), ("A", "adj_k", 23.0), ("A", "logit_row", 26.0),
    ("A", "softmax", 27.0), ("A", "value", 28.0), ("A", "prob_col", 31.0),
    ("B", "norm2", 1.5), ("B", "turn2", 6.0), ("B", "sup1", 9.0), ("B", "hid1", 13.0), ("B", "sup2", 17.0),
    ("B", "hid2", 21.0), ("B", "sup3", 25.0), ("B", "gcn", 29.0),
    ("C", "norm3", -1.0), ("C", "turn3", 3.0), ("C", "att_cols", 5.0), ("C", "diff_y", 7.0), ("C", "att_rows", 8.5),
    ("C", "leaky", 10.0), ("C", "alpha", 11.5), ("C", "trans", 15.0), ("C", "diff_z", 18.0), ("C", "diffuse", 23.0),
]
PAIR_SHIFT = 3.0
NO_PRODUCTS = ("norm0", "norm1", "norm2", "norm3", "softmax", "leaky", "alpha")
ORDER = [(phase, step, p) for _, phase, step, p in
         sorted((at + PAIR_SHIFT * p, phase, step, p) for phase, step, at in PLACES for p in range(2))]
PE_ORDER = [x for x in ORDER if x[1] not in NO_PRODUCTS]


def build(nc, x, adj, adj_t, w0_t, wqk_t, wv_t, w1, w2, w3, b12, b3, att_w, att_b, att_vec, att_c, wk, bk, out):
    graphs, nodes, feat = x.shape
    att = wqk_t.shape[1] // 2
    hops = wk.shape[0]
    pairs = graphs // 2
    groups = pairs // 2
    assert nodes == P and feat == 2 * P and hops == 3
    fc = feat // P

    x_d = x.rearrange("(j g) n d -> j n g d", g=2)
    adj_d = adj.rearrange("(j g) n m -> j n g m", g=2)
    adj_t_d = adj_t.rearrange("(j g) m n -> j m g n", g=2)
    out_d = out.rearrange("(j g) n d -> j n g d", g=2)

    with ExitStack() as ctx:
        def sb(name, shape, dt=F32):
            return ctx.enter_context(nc.sbuf_tensor(name, shape, dt))

        def pair_buf(name, shape, dt=F32):
            return [sb(f"{name}_p{p}", shape, dt) for p in range(2)]

        def split_buf(name, shape):
            return [(sb(f"{name}_hi_p{p}", shape, F32R), sb(f"{name}_lo_p{p}", shape, F32R)) for p in range(2)]

        def weight(name, cols):
            return sb(f"{name}_hi", [P, fc, cols], F32R), sb(f"{name}_lo", [P, fc, cols], F32R)

        w_self, w_agg = weight("w_self", feat), weight("w_agg", feat)
        w_qk, w_val = weight("w_qk", 2 * att), weight("w_val", feat)
        w_gcn = [weight(f"w_gcn{i}", feat) for i in range(3)]
        w_hop = [weight(f"w_hop{i}", feat) for i in range(hops)]
        w_att = weight("w_att", 2)
        ident = sb("ident", [P, P])
        minus_half = sb("minus_half", [P, 2])
        bias_hid = sb("bias_hid", [P, 2, fc])
        bias_gcn = sb("bias_gcn", [P, feat])
        bias_hops = sb("bias_hops", [P, hops, feat])
        bias_diff = sb("bias_diff", [P, feat])
        att_bias = sb("att_bias", [P, 4])
        att_stage = sb("att_stage", [P, fc, feat])
        att_rows_w = sb("att_rows_w", [P, 2, feat])
        att_b_row = sb("att_b_row", [P, feat])
        att_cols_w = sb("att_cols_w", [P, fc, 2])

        x0 = pair_buf("x0", [P, 2, feat])
        x1 = pair_buf("x1", [P, 2, feat])
        x2 = pair_buf("x2", [P, 2, feat])
        x3 = pair_buf("x3", [P, 2, feat])
        x2_bias = pair_buf("x2_bias", [P, 2, feat])
        x3_kept = pair_buf("x3_kept", [P, 2, feat])
        y = pair_buf("y", [P, 2, feat])
        stats = [pair_buf(f"stats{l}", [P, 2, 6]) for l in range(4)]
        mean_var = [pair_buf(f"mean_var{l}", [P, 2, 2]) for l in range(4)]
        var_eps = [pair_buf(f"var_eps{l}", [P, 2]) for l in range(4)]
        rstd = [pair_buf(f"rstd{l}", [P, 2]) for l in range(4)]
        z = [pair_buf(f"z{l}", [P, 2, feat]) for l in range(4)]
        hT_a = split_buf("hT_a", [P, 2, fc, P])
        hT_b = split_buf("hT_b", [P, 2, fc, P])
        hT_c = split_buf("hT_c", [P, 2, fc, P])
        adj_a = pair_buf("adj_a", [P, 2, P])
        adj_c = pair_buf("adj_c", [P, 2, P])
        adjT_a_in = pair_buf("adjT_a_in", [P, 2, P])
        adjT_b_in = pair_buf("adjT_b_in", [P, 2, P])
        adjT_a = split_buf("adjT_a", [P, 2, P])
        adjT_b = split_buf("adjT_b", [P, 2, P])
        deg = pair_buf("deg", [P, 2])
        deg_floor = pair_buf("deg_floor", [P, 2])
        deg_inv = pair_buf("deg_inv", [P, 2])
        adj_n = pair_buf("adj_n", [P, 2, P])
        adjT_n = split_buf("adjT_n", [P, 2, P])
        sage_y = split_buf("sage_y", [P, 2, feat])
        q = pair_buf("q", [P, 2, att])
        key = split_buf("key", [P, 2, att])
        qk_prod = pair_buf("qk_prod", [P, 2, att])
        logit = pair_buf("logit", [P, 2])
        logit_max = pair_buf("logit_max", [2, 1])
        exp_bias = pair_buf("exp_bias", [2, 1])
        prob = pair_buf("prob", [2, P])
        prob_sum = pair_buf("prob_sum", [2, 1])
        prob_inv = pair_buf("prob_inv", [2, 1])
        prob_n = pair_buf("prob_n", [2, P])
        prob_col = pair_buf("prob_col", [P, 2])
        sup = split_buf("sup", [P, 2, feat])
        hid = pair_buf("hid", [P, fc, 2, P])
        hidT = split_buf("hidT", [P, fc, 2, P])
        att_col = pair_buf("att_col", [P, 2, 2])
        pair_score = pair_buf("pair_score", [P, 2, P])
        leaky = pair_buf("leaky", [P, 2, P])
        expo = pair_buf("expo", [P, 2, P])
        alpha = pair_buf("alpha", [P, 2, P])
        row_sum = pair_buf("row_sum", [P, 2])
        row_inv = pair_buf("row_inv", [P, 2])
        trans = pair_buf("trans", [P, 2, P])
        transT = split_buf("transT", [P, 2, P])
        diff = split_buf("diff", [P, 2, feat])

        stage = [*x2_bias, *z[2], *y, *x3_kept, *z[3]]

        bank = [ctx.enter_context(nc.psum_tensor(f"bank{i}", [P, 512], F32)) for i in range(BANKS)]

        def sem(name):
            return ctx.enter_context(nc.semaphore(name))

        def each(names):
            return {name: sem(name) for name in names.split()}

        mm = {s: sem(f"{s}_mm") for _, s, _ in PLACES if s not in NO_PRODUCTS}
        hi = {s: sem(f"{s}_hi") for s in
              "adj_norm turn0 sage_y turn1 qk turn2 sup1 hid1 sup2 hid2 sup3 turn3 diff_y trans diff_z".split()}
        read = {s: sem(f"{s}_read") for s in mm}
        got = each("stats0 stats1 stats2 stats3 moments0 moments1 moments2 moments3 var_eps0 var_eps1 var_eps2 "
                   "var_eps3 rstd0 rstd1 rstd2 rstd3 z0 z1 z2 z3 deg deg_floor deg_inv adj_n adjT_a_hi adjT_a "
                   "adjT_b_hi adjT_b q logit_max exp_bias prob prob_inv prob_n prob_col x2 x2_bias x3_kept "
                   "hid1_half hid2_half leaky expo alpha row_inv trans diff_sum y")
        landed = {name: [sem(f"{name}_landed_p{p}") for p in range(2)]
                  for name in "x0 adj_a adjT_a adjT_b adj_c out".split()}
        w_landed = [sem(f"w_landed{i}") for i in range(10)]
        small_landed = sem("small_landed")
        w_hi, w_lo = sem("w_hi"), sem("w_lo")
        const_made = sem("const_made")
        att_made = sem("att_made")
        bias_made = sem("bias_made")

        def active(phase, t):
            return not isinstance(t, int) or 0 <= t - PHASE_LAG[phase] < groups

        def run(eng, steps, order, between=None):
            def one(t):
                for phase, step, p in order:
                    if active(phase, t) and step in steps:
                        steps[step](t, (t - PHASE_LAG[phase]) * 2 + (p + 1), p)

            warm = max(PHASE_LAG.values()) + 1
            for t in range(warm):
                one(t)
                if between:
                    between(t)
            with eng.Fori(warm, groups) as t:
                one(t)
            for t in range(groups, groups + warm - 1):
                one(t)

        def before(n):
            return None if isinstance(n, int) and n <= 2 else n - 2

        block = ctx.enter_context(nc.Block())

        w_sources = [
            (w0_t[feat:2 * feat, :], w_agg), (w0_t[0:feat, :], w_self), (wqk_t, w_qk), (wv_t, w_val),
            (w1, w_gcn[0]), (w2, w_gcn[1]), (w3, w_gcn[2]), (wk[2], w_hop[2]), (wk[1], w_hop[1]), (wk[0], w_hop[0]),
        ]
        W_OF_PHASE = {"A": (0, 4), "B": (4, 7), "C": (7, 10)}
        W_ATT = 11

        @block.sync
        def _(sp):
            def load(name, dst, src, reader, n, p):
                if before(n) is not None:
                    sp.wait_ge(reader, before(n))
                sp.dma_start(dst[p][:], src[n - 1]).then_inc(landed[name][p], 16)

            def first_loads(t, n, p):
                load("adj_a", adj_a, adj_d, got["adj_n"], n, p)
                load("x0", x0, x_d, read["sage"], n, p)
                load("adjT_a", adjT_a_in, adj_t_d, got["adjT_a"], n, p)

            def gcn_load(t, n, p):
                load("adjT_b", adjT_b_in, adj_t_d, got["adjT_b"], n, p)

            def diffusion_load(t, n, p):
                load("adj_c", adj_c, adj_d, got["alpha"], n, p)

            def store(t, n, p):
                sp.wait_ge(got["y"], n)
                sp.dma_start(out_d[n - 1], y[p][:]).then_inc(landed["out"][p], 16)

            def weights(i):
                src, (half, _) = w_sources[i]
                cols = half.shape[2]
                sp.dma_start(stage[i][:, :, 0:cols], src.rearrange("(c p) o -> p c o", p=P)).then_inc(w_landed[i], 16)

            first_loads(0, 1, 0)
            weights(0)
            first_loads(0, 2, 1)
            for i in range(1, len(w_sources)):
                weights(i)
            small = [
                (bias_hid[:], b12),
                (bias_gcn[:], b3.partition_broadcast(P)),
                (bias_hops[:], bk.partition_broadcast(P)),
                (att_stage[:], att_w.rearrange("(c p) o -> p c o", p=P)),
                (att_rows_w[:], att_vec.rearrange("(s d) o -> (o s) d", s=2).partition_broadcast(P)),
                (att_b_row[:], att_b.partition_broadcast(P)),
                (att_bias[:, 0:1], att_c.partition_broadcast(P)),
            ]
            assert len(small) == SMALL_LOADS
            for dst, src in small:
                sp.dma_start(dst, src).then_inc(small_landed, 16)

            steps = {"turn3": diffusion_load, "turn2": gcn_load, "diffuse": store}
            order = [o for o in ORDER if o[1] in steps]

            def one(t):
                for phase, step, p in order:
                    if active(phase, t):
                        steps[step](t, (t - PHASE_LAG[phase]) * 2 + (p + 1), p)

            def next_a(t):
                for p in range(2):
                    first_loads(t, t * 2 + (p + 1), p)

            warm = max(PHASE_LAG.values()) + 1
            for t in range(warm):
                if t > 0:
                    next_a(t)
                one(t)
            with sp.Fori(warm, groups) as t:
                next_a(t)
                one(t)
            for t in range(groups, groups + warm - 1):
                one(t)
            for p in range(2):
                sp.wait_ge(landed["out"][p], 16 * groups)

        @block.gpsimd
        def _(pool):
            nc.gpsimd.memset(ident[:], 0.0).then_inc(const_made, 1)
            pool.wait_ge(const_made, 1)
            nc.gpsimd.affine_select(out=ident[:], in_=ident[:], compare_op=ALU.not_equal, fill=1.0, base=0,
                                    pattern=[[-1, P]], channel_multiplier=1).then_inc(const_made, 1)
            nc.gpsimd.memset(minus_half[:], -0.5).then_inc(const_made, 1)
            pool.wait_ge(const_made, 3)

            def normalize(l, src, transposed, n, p):
                pool.wait_ge(got[f"moments{l}"], n)
                pool.nop(nofuse=True)
                nc.gpsimd.tensor_scalar(var_eps[l][p][:], mean_var[l][p][:, :, 1], LAYERNORM_EPS, None,
                                        ALU.add).then_inc(got[f"var_eps{l}"], 1)
                pool.wait_ge(got[f"var_eps{l}"], n)
                nc.gpsimd.tensor_tensor(rstd[l][p][:], var_eps[l][p][:], minus_half[:],
                                        ALU.pow).then_inc(got[f"rstd{l}"], 1)
                pool.wait_ge(got[f"rstd{l}"], n)
                if before(n) is not None:
                    pool.wait_ge(mm[transposed], before(n))
                pool.nop(nofuse=True)
                for g in range(2):
                    last = nc.gpsimd.tensor_scalar(z[l][p][:, g, :], src[p][:, g, :], mean_var[l][p][:, g, 0:1],
                                                   rstd[l][p][:, g:g + 1], ALU.subtract, ALU.mult)
                last.then_inc(got[f"z{l}"], 1)

            def split_adj(name, src, halves, last_user, n, p):
                pool.wait_ge(landed[name][p], ((n + (1 - p)) // 2) * 16 if isinstance(n, int) else (n + (1 - p)) * 8)
                if before(n) is not None:
                    pool.wait_ge(last_user, before(n))
                h, l = halves[p]
                pool.nop(nofuse=True)
                nc.gpsimd.tensor_copy(h[:], src[p][:]).then_inc(got[f"{name}_hi"], 1)
                pool.wait_ge(got[f"{name}_hi"], n)
                nc.gpsimd.tensor_tensor(l[:], src[p][:], h[:].bitcast(F32), ALU.subtract).then_inc(got[name], 1)

            def norm0(t, n, p):
                normalize(0, x0, "turn0", n, p)
                pool.wait_ge(got["deg_inv"], n)
                if before(n) is not None:
                    pool.wait_ge(mm["adj_norm"], before(n))
                pool.nop(nofuse=True)
                for g in range(2):
                    last = nc.gpsimd.tensor_scalar(adj_n[p][:, g, :], adj_a[p][:, g, :], deg_inv[p][:, g:g + 1], None,
                                                   ALU.mult)
                last.then_inc(got["adj_n"], 1)

            def norm1(t, n, p):
                normalize(1, x1, "turn1", n, p)
                split_adj("adjT_a", adjT_a_in, adjT_a, mm["adj_k"], n, p)

            def norm2(t, n, p):
                normalize(2, x2, "turn2", n, p)
                if before(n) is not None:
                    pool.wait_ge(read["gcn"], before(n))
                if isinstance(n, int) and n == 1:
                    pool.wait_ge(small_landed, 16 * SMALL_LOADS)
                nc.gpsimd.tensor_tensor(x2_bias[p][:], x2[p][:], bias_gcn[:].unsqueeze(1).to_broadcast([P, 2, feat]),
                                        ALU.add).then_inc(got["x2_bias"], 1)

            def turn2(t, n, p):
                split_adj("adjT_b", adjT_b_in, adjT_b, mm["gcn"], n, p)

            def norm3(t, n, p):
                normalize(3, x3, "turn3", n, p)
                if before(n) is not None:
                    pool.wait_ge(got["y"], before(n))
                pool.nop(nofuse=True)
                nc.gpsimd.tensor_copy(x3_kept[p][:], x3[p][:]).then_inc(got["x3_kept"], 1)

            def split_hidden(step):
                def do(t, n, p):
                    pool.wait_ge(read[step], n)
                    h, l = hidT[p]
                    pool.nop(nofuse=True)
                    nc.gpsimd.tensor_copy(h[:], hid[p][:]).then_inc(hi[step], 1)
                    pool.wait_ge(hi[step], n)
                    nc.gpsimd.tensor_tensor(l[:], hid[p][:], h[:].bitcast(F32),
                                            ALU.subtract).then_inc(got[f"{step}_half"], 1)
                return do

            def alpha_rows(t, n, p):
                pool.wait_ge(got["row_inv"], n)
                if before(n) is not None:
                    pool.wait_ge(mm["trans"], before(n))
                pool.nop(nofuse=True)
                for g in range(2):
                    last = nc.gpsimd.tensor_scalar(trans[p][:, g, :], alpha[p][:, g, :], row_inv[p][:, g:g + 1], None,
                                                   ALU.mult)
                last.then_inc(got["trans"], 1)

            run(pool, {"norm0": norm0, "norm1": norm1, "norm2": norm2, "turn2": turn2, "norm3": norm3,
                       "hid1": split_hidden("hid1"), "hid2": split_hidden("hid2"), "alpha": alpha_rows}, ORDER)

        bank_of = {(step, p): bank[i % BANKS] for i, (_, step, p) in enumerate(PE_ORDER)}
        assert len(PE_ORDER) % BANKS == 0

        def view(step, p, *dims):
            size = 1
            for d in dims:
                size *= d
            b = bank_of[step, p][:, 0:size]
            if len(dims) == 2:
                return b.rearrange("p (a b) -> p a b", b=dims[1])
            if len(dims) == 3:
                return b.rearrange("p (a b c) -> p a b c", b=dims[1], c=dims[2])
            return b

        @block.scalar
        def _(act):
            def weights(phase):
                for i in range(*W_OF_PHASE[phase]):
                    half = w_sources[i][1][0]
                    act.wait_ge(w_landed[i], 16)
                    nc.scalar.activation(half[:], stage[i][:, :, 0:half.shape[2]], ACT.Copy).then_inc(w_hi, 1)
                if phase == "C":
                    act.wait_ge(att_made, 4)
                    nc.scalar.activation(w_att[0][:], att_cols_w[:], ACT.Copy).then_inc(w_hi, 1)

            def take_hi(step, halves, func, *dims):
                def do(t, n, p):
                    act.wait_ge(mm[step], n)
                    nc.scalar.activation(halves[p][0][:], view(step, p, *dims), func).then_inc(hi[step], 1)
                return do

            def qk(t, n, p):
                act.wait_ge(mm["qk"], n)
                v = view("qk", p, 2, 2 * att)
                nc.scalar.activation(key[p][0][:], v[:, :, att:2 * att], ACT.Copy).then_inc(hi["qk"], 1)
                if before(n) is not None:
                    act.wait_ge(read["adj_k"], before(n))
                nc.scalar.activation(q[p][:], v[:, :, 0:att], ACT.Copy).then_inc(got["q"], 1)

            def softmax(t, n, p):
                act.wait_ge(got["exp_bias"], n)
                if before(n) is not None:
                    act.wait_ge(got["prob_n"], before(n))
                nc.scalar.activation(prob[p][:], view("logit_row", p, P)[0:2, :], ACT.Exp, bias=exp_bias[p][:, 0:1],
                                     scale=float(att) ** -0.5, accum_out=prob_sum[p][:, 0:1]).then_inc(got["prob"], 1)

            def hidden(step, layer):
                def do(t, n, p):
                    act.wait_ge(mm[step], n)
                    if step == "hid2":
                        act.wait_ge(got["hid1_half"], n)
                    elif before(n) is not None:
                        act.wait_ge(got["hid2_half"], before(n))
                    v = view(step, p, fc, 2, P)
                    for c in range(fc):
                        last = nc.scalar.activation(hid[p][:, c], v[:, c], ACT.Relu,
                                                    bias=bias_hid[:, layer, c:c + 1])
                    last.then_inc(read[step], 1)
                return do

            def att_rows(t, n, p):
                act.wait_ge(mm["att_rows"], n)
                v = view("att_rows", p, 2, P)
                if before(n) is not None:
                    act.wait_ge(got["leaky"], before(n))
                for g in range(2):
                    last = nc.scalar.activation(pair_score[p][:, g, :], v[:, g, :], ACT.Identity,
                                                bias=att_col[p][:, g, 1:2])
                last.then_inc(read["att_rows"], 1)

            def exponent(t, n, p):
                act.wait_ge(got["leaky"], n)
                if before(n) is not None:
                    act.wait_ge(got["alpha"], before(n))
                nc.scalar.activation(expo[p][:], leaky[p][:], ACT.Exp).then_inc(got["expo"], 1)

            weights("A")
            act.wait_ge(small_landed, 16 * SMALL_LOADS)
            run(act, {
                "adj_norm": take_hi("adj_norm", adjT_n, ACT.Copy, 2, P),
                "turn0": take_hi("turn0", hT_a, ACT.Relu, 2, fc, P),
                "sage_y": take_hi("sage_y", sage_y, ACT.Copy, 2, feat),
                "turn1": take_hi("turn1", hT_a, ACT.Relu, 2, fc, P),
                "qk": qk, "softmax": softmax,
                "turn2": take_hi("turn2", hT_b, ACT.Relu, 2, fc, P),
                "sup1": take_hi("sup1", sup, ACT.Copy, 2, feat),
                "hid1": hidden("hid1", 0),
                "sup2": take_hi("sup2", sup, ACT.Copy, 2, feat),
                "hid2": hidden("hid2", 1),
                "sup3": take_hi("sup3", sup, ACT.Copy, 2, feat),
                "turn3": take_hi("turn3", hT_c, ACT.Relu, 2, fc, P),
                "diff_y": take_hi("diff_y", diff, ACT.Copy, 2, feat),
                "att_rows": att_rows, "leaky": exponent,
                "trans": take_hi("trans", transT, ACT.Copy, 2, P),
                "diff_z": take_hi("diff_z", diff, ACT.Copy, 2, feat),
            }, ORDER, lambda t: weights("BC"[t]) if t < 2 else None)

        @block.vector
        def _(dve):
            def weights(phase):
                for i in range(*W_OF_PHASE[phase]):
                    h, l = w_sources[i][1]
                    dve.wait_ge(w_hi, i + 1)
                    nc.vector.tensor_tensor(l[:], stage[i][:, :, 0:h.shape[2]], h[:].bitcast(F32),
                                            ALU.subtract).then_inc(w_lo, 1)
                if phase == "B":
                    attention_weights()
                    for i in range(1, hops):
                        other = bias_hops[:, 0, :] if i == 1 else bias_diff[:]
                        if i > 1:
                            dve.wait_ge(bias_made, i - 1)
                        nc.vector.tensor_tensor(bias_diff[:], other, bias_hops[:, i, :],
                                                ALU.add).then_inc(bias_made, 1)
                if phase == "C":
                    dve.wait_ge(w_hi, W_ATT)
                    nc.vector.tensor_tensor(w_att[1][:], att_cols_w[:], w_att[0][:].bitcast(F32),
                                            ALU.subtract).then_inc(w_lo, 1)

            def attention_weights():
                junk = leaky[0][:].rearrange("p g m -> p (g m)")
                dve.wait_ge(small_landed, 16 * SMALL_LOADS)
                for c in range(fc):
                    for s in range(2):
                        nc.vector.tensor_tensor_reduce(junk, att_stage[:, c, :], att_rows_w[:, s, :], 1.0,
                                                       0.0, ALU.mult, ALU.add,
                                                       att_cols_w[:, c, s:s + 1]).then_inc(att_made, 1)
                        dve.wait_ge(att_made, fc * c + s + 1)
                for s in range(2):
                    nc.vector.tensor_tensor_reduce(junk, att_b_row[:], att_rows_w[:, s, :], 1.0, 0.0,
                                                   ALU.mult, ALU.add, att_bias[:, s + 1:s + 2]).then_inc(att_made, 1)
                    dve.wait_ge(att_made, 2 * fc + s + 1)
                nc.vector.reduce_sum(att_bias[:, 3:4], att_bias[:, 0:3], AX_X).then_inc(att_made, 1)

            def moments(l, src, n, p):
                for g in range(2):
                    last = nc.vector.bn_stats(stats[l][p][:, g, :], src[p][:, g, :])
                last.then_inc(got[f"stats{l}"], 1)
                dve.wait_ge(got[f"stats{l}"], n)
                if before(n) is not None:
                    dve.wait_ge(got[f"z{l}"], before(n))
                dve.nop(nofuse=True)
                for g in range(2):
                    last = nc.vector.bn_aggr(mean_var[l][p][:, g, :], stats[l][p][:, g, :])
                last.then_inc(got[f"moments{l}"], 1)

            def landed_count(n, p):
                return (n + (1 - p)) // 2 * 16 if isinstance(n, int) else (n + (1 - p)) * 8

            def norm0(t, n, p):
                dve.wait_ge(landed["x0"][p], landed_count(n, p))
                moments(0, x0, n, p)
                dve.wait_ge(landed["adj_a"][p], landed_count(n, p))
                nc.vector.reduce_sum(deg[p][:], adj_a[p][:], AX_X).then_inc(got["deg"], 1)
                dve.wait_ge(got["deg"], n)
                nc.vector.tensor_scalar(deg_floor[p][:], deg[p][:], DEGREE_EPS, None,
                                        ALU.max).then_inc(got["deg_floor"], 1)
                dve.wait_ge(got["deg_floor"], n)
                if before(n) is not None:
                    dve.wait_ge(got["adj_n"], before(n))
                nc.vector.reciprocal(deg_inv[p][:], deg_floor[p][:]).then_inc(got["deg_inv"], 1)

            def take_lo(step, halves, *dims):
                def do(t, n, p):
                    h, l = halves[p]
                    dve.wait_ge(hi[step], n)
                    nc.vector.tensor_tensor(l[:], view(step, p, *dims), h[:].bitcast(F32),
                                            ALU.subtract).then_inc(read[step], 1)
                return do

            def take_relu_lo(step, halves):
                def do(t, n, p):
                    h, l = halves[p]
                    dve.wait_ge(hi[step], n)
                    b = bank_of[step, p][:]
                    nc.vector.scalar_tensor_tensor(l[:].rearrange("p a b c -> p (a b c)"), b, 0.0,
                                                   h[:].bitcast(F32).rearrange("p a b c -> p (a b c)"), ALU.max,
                                                   ALU.subtract).then_inc(read[step], 1)
                return do

            def sage(t, n, p):
                dve.wait_ge(mm["sage"], n)
                if before(n) is not None:
                    dve.wait_ge(read["value"], before(n))
                    dve.wait_ge(got["z1"], before(n))
                nc.vector.scalar_tensor_tensor(x1[p][:], view("sage", p, 2, feat), 0.0, x0[p][:], ALU.max,
                                               ALU.add).then_inc(read["sage"], 1)

            def norm1(t, n, p):
                dve.wait_ge(read["sage"], n)
                moments(1, x1, n, p)

            def qk(t, n, p):
                dve.wait_ge(hi["qk"], n)
                dve.wait_ge(got["q"], n)
                nc.vector.tensor_tensor(key[p][1][:], view("qk", p, 2, 2 * att)[:, :, att:2 * att],
                                        key[p][0][:].bitcast(F32), ALU.subtract).then_inc(read["qk"], 1)

            def adj_k(t, n, p):
                dve.wait_ge(mm["adj_k"], n)
                if before(n) is not None:
                    dve.wait_ge(mm["logit_row"], before(n))
                v = view("adj_k", p, 2, att)
                for g in range(2):
                    last = nc.vector.tensor_tensor_reduce(qk_prod[p][:, g, :], v[:, g, :], q[p][:, g, :], 1.0, 0.0,
                                                          ALU.mult, ALU.add, logit[p][:, g:g + 1])
                last.then_inc(read["adj_k"], 1)

            def logit_row(t, n, p):
                dve.wait_ge(mm["logit_row"], n)
                nc.vector.reduce_max(logit_max[p][:], view("logit_row", p, P)[0:2, :],
                                     AX_X).then_inc(got["logit_max"], 1)
                dve.wait_ge(got["logit_max"], n)
                if before(n) is not None:
                    dve.wait_ge(got["prob"], before(n))
                nc.vector.tensor_scalar(exp_bias[p][:], logit_max[p][:], -float(att) ** -0.5, None,
                                        ALU.mult).then_inc(got["exp_bias"], 1)

            def value(t, n, p):
                dve.wait_ge(got["prob"], n)
                nc.vector.reciprocal(prob_inv[p][:], prob_sum[p][:]).then_inc(got["prob_inv"], 1)
                dve.wait_ge(got["prob_inv"], n)
                if before(n) is not None:
                    dve.wait_ge(mm["prob_col"], before(n))
                nc.vector.tensor_scalar(prob_n[p][:], prob[p][:], prob_inv[p][:, 0:1], None,
                                        ALU.mult).then_inc(got["prob_n"], 1)

            def prob_column(t, n, p):
                dve.wait_ge(mm["prob_col"], n)
                nc.vector.tensor_copy(prob_col[p][:], view("prob_col", p, 2)).then_inc(read["prob_col"], 1)
                dve.wait_ge(read["prob_col"], n)
                dve.wait_ge(mm["value"], n)
                if before(n) is not None:
                    dve.wait_ge(got["z2"], before(n))
                    dve.wait_ge(got["x2_bias"], before(n))
                v = view("value", p, 2, feat)
                nc.vector.scalar_tensor_tensor(x2[p][:, 0, :], v[:, 0, :], prob_col[p][:, 0:1], x1[p][:, 0, :],
                                               ALU.mult, ALU.add)
                nc.vector.scalar_tensor_tensor(x2[p][:, 1, :], v[:, 1, :], prob_col[p][:, 1:2], x1[p][:, 1, :],
                                               ALU.mult, ALU.add).then_inc(read["value"], 1)

            def norm2(t, n, p):
                dve.wait_ge(read["value"], n)
                moments(2, x2, n, p)

            def gcn(t, n, p):
                dve.wait_ge(mm["gcn"], n)
                dve.wait_ge(got["x2_bias"], n)
                if before(n) is not None:
                    dve.wait_ge(got["z3"], before(n))
                    dve.wait_ge(got["x3_kept"], before(n))
                nc.vector.tensor_tensor(x3[p][:], view("gcn", p, 2, feat), x2_bias[p][:],
                                        ALU.add).then_inc(read["gcn"], 1)

            def norm3(t, n, p):
                dve.wait_ge(read["gcn"], n)
                moments(3, x3, n, p)

            def att_cols(t, n, p):
                dve.wait_ge(mm["att_cols"], n)
                v = view("att_cols", p, 2, 2)
                if before(n) is not None:
                    dve.wait_ge(read["att_rows"], before(n))
                nc.vector.tensor_copy(att_col[p][:, :, 0], v[:, :, 0])
                nc.vector.tensor_scalar(att_col[p][:, :, 1], v[:, :, 1], att_bias[:, 3:4], None,
                                        ALU.add).then_inc(read["att_cols"], 1)

            def leaky_relu(t, n, p):
                dve.wait_ge(read["att_rows"], n)
                if before(n) is not None:
                    dve.wait_ge(got["expo"], before(n))
                s = pair_score[p][:]
                nc.vector.scalar_tensor_tensor(leaky[p][:], s, LEAKY_SLOPE, s, ALU.mult,
                                               ALU.max).then_inc(got["leaky"], 1)

            def alpha_rows(t, n, p):
                dve.wait_ge(landed["adj_c"][p], landed_count(n, p))
                dve.wait_ge(got["expo"], n)
                if before(n) is not None:
                    dve.wait_ge(got["trans"], before(n))
                for g in range(2):
                    last = nc.vector.tensor_tensor_reduce(alpha[p][:, g, :], adj_c[p][:, g, :], expo[p][:, g, :], 1.0,
                                                          ROW_SUM_EPS, ALU.mult, ALU.add, row_sum[p][:, g:g + 1])
                last.then_inc(got["alpha"], 1)
                dve.wait_ge(got["alpha"], n)
                nc.vector.reciprocal(row_inv[p][:], row_sum[p][:]).then_inc(got["row_inv"], 1)

            def diffuse(t, n, p):
                dve.wait_ge(mm["diffuse"], n)
                if before(n) is not None:
                    dve.wait_ge(landed["out"][p], landed_count(n, p) - 16)
                nc.vector.tensor_tensor(y[p][:], view("diffuse", p, 2, feat),
                                        bias_diff[:].unsqueeze(1).to_broadcast([P, 2, feat]),
                                        ALU.add).then_inc(read["diffuse"], 1)
                dve.wait_ge(read["diffuse"], n)
                dve.wait_ge(got["x3_kept"], n)
                nc.vector.scalar_tensor_tensor(y[p][:], y[p][:], 0.0, x3_kept[p][:], ALU.max,
                                               ALU.add).then_inc(got["y"], 1)

            weights("A")
            run(dve, {
                "norm0": norm0, "norm1": norm1, "norm2": norm2, "norm3": norm3,
                "adj_norm": take_lo("adj_norm", adjT_n, 2, P),
                "turn0": take_relu_lo("turn0", hT_a), "turn1": take_relu_lo("turn1", hT_a),
                "turn2": take_relu_lo("turn2", hT_b), "turn3": take_relu_lo("turn3", hT_c),
                "sage_y": take_lo("sage_y", sage_y, 2, feat), "sage": sage, "qk": qk, "adj_k": adj_k,
                "logit_row": logit_row, "value": value, "prob_col": prob_column,
                "sup1": take_lo("sup1", sup, 2, feat), "sup2": take_lo("sup2", sup, 2, feat),
                "sup3": take_lo("sup3", sup, 2, feat), "gcn": gcn,
                "att_cols": att_cols, "leaky": leaky_relu, "alpha": alpha_rows, "trans": take_lo("trans", transT, 2, P),
                "diff_y": take_lo("diff_y", diff, 2, feat), "diff_z": take_lo("diff_z", diff, 2, feat),
                "diffuse": diffuse,
            }, ORDER, lambda t: weights("BC"[t]) if t < 2 else None)

        @block.tensor
        def _(pe):
            def free_bank(t, step, p):
                at, back = [(s, q) for _, s, q in PE_ORDER].index((step, p)), 0
                while True:
                    at -= BANKS
                    if at < 0:
                        at, back = at + len(PE_ORDER), back + 1
                    phase, user, q = PE_ORDER[at]
                    if isinstance(t, int) and t < back:
                        return
                    if active(phase, t - back if isinstance(t, int) else t):
                        break
                user_read = got["prob"] if user == "logit_row" else read[user]
                pe.wait_ge(user_read, (t - back - PHASE_LAG[phase]) * 2 + (q + 1))

            def product(out_ap, left, right, start=True, stop=True):
                (lh, ll), (rh, rl) = left, right
                nc.tensor.matmul(out_ap, lh, rl, start=start, stop=False, skip_group_check=True)
                nc.tensor.matmul(out_ap, ll, rh, start=False, stop=False, skip_group_check=True)
                return nc.tensor.matmul(out_ap, lh, rh, start=False, stop=stop, skip_group_check=True)

            def pick(halves, *index):
                return tuple(h[(slice(None), *index)] for h in halves)

            def turn(step, l):
                def do(t, n, p):
                    free_bank(t, step, p)
                    pe.wait_ge(got[f"z{l}"], n)
                    v = view(step, p, 2, fc, P)
                    for g in range(2):
                        for c in range(fc):
                            last = nc.tensor.transpose(v[:, g, c, :], z[l][p][:, g, c * P:(c + 1) * P], ident[:])
                    last.then_inc(mm[step], 1)
                return do

            def turn_rows(step, src, ready):
                def do(t, n, p):
                    free_bank(t, step, p)
                    pe.wait_ge(got[ready], n)
                    v = view(step, p, 2, P)
                    for g in range(2):
                        last = nc.tensor.transpose(v[:, g, :], src[p][:, g, :], ident[:])
                    last.then_inc(mm[step], 1)
                return do

            def project(step, actT, ready, w, cols):
                def do(t, n, p):
                    free_bank(t, step, p)
                    pe.wait_ge(ready, n)
                    v = view(step, p, 2, cols)
                    for g in range(2):
                        for c in range(fc):
                            last = product(v[:, g, :], pick(actT[p], g, c), pick(w, c), start=c == 0,
                                           stop=c == fc - 1)
                    last.then_inc(mm[step], 1)
                return do

            def project_hidden(step, ready, w):
                def do(t, n, p):
                    free_bank(t, step, p)
                    pe.wait_ge(ready, n)
                    v = view(step, p, 2, feat)
                    for g in range(2):
                        for c in range(fc):
                            last = product(v[:, g, :], pick(hidT[p], c, g), pick(w, c), start=c == 0,
                                           stop=c == fc - 1)
                    last.then_inc(mm[step], 1)
                return do

            def project_and_spread(step, actT, ready, w, nodesT, moved, moved_ready):
                def do(t, n, p):
                    free_bank(t, step, p)
                    pe.wait_ge(ready, n)
                    v = view(step, p, 2, feat)
                    for g in range(2):
                        for c in range(fc):
                            product(v[:, g, :], pick(actT[p], g, c), pick(w, c), start=g == 0 and c == 0, stop=False)
                    for r in moved_ready:
                        pe.wait_ge(r, n)
                    for g in range(2):
                        last = product(v[:, g, :], pick(nodesT[p], g), pick(moved[p], g), start=False, stop=True)
                    last.then_inc(mm[step], 1)
                return do

            def spread(step, nodesT, moved, cols, ready):
                def do(t, n, p):
                    free_bank(t, step, p)
                    for r in ready:
                        pe.wait_ge(r, n)
                    v = view(step, p, 2, cols)
                    for g in range(2):
                        last = product(v[:, g, :], pick(nodesT[p], g), pick(moved[p], g))
                    last.then_inc(mm[step], 1)
                return do

            def spread_hidden(step, ready):
                def do(t, n, p):
                    free_bank(t, step, p)
                    pe.wait_ge(ready, n)
                    pe.wait_ge(got["adjT_b"], n)
                    v = view(step, p, fc, 2, P)
                    for g in range(2):
                        for c in range(fc):
                            last = product(v[:, c, g, :], pick(sup[p], g, slice(c * P, (c + 1) * P)),
                                           pick(adjT_b[p], g))
                    last.then_inc(mm[step], 1)
                return do

            def logit_row(t, n, p):
                free_bank(t, "logit_row", p)
                pe.wait_ge(read["adj_k"], n)
                nc.tensor.matmul(view("logit_row", p, P)[0:2, :], logit[p][:], ident[:], start=True,
                                 stop=True).then_inc(mm["logit_row"], 1)

            def prob_column(t, n, p):
                free_bank(t, "prob_col", p)
                pe.wait_ge(got["prob_n"], n)
                nc.tensor.matmul(view("prob_col", p, 2), prob_n[p][:], ident[0:2, 0:2], start=True,
                                 stop=True).then_inc(mm["prob_col"], 1)

            def att_rows(t, n, p):
                free_bank(t, "att_rows", p)
                pe.wait_ge(read["att_cols"], n)
                v = view("att_rows", p, 2, P)
                for g in range(2):
                    last = nc.tensor.transpose(v[:, g, :], att_col[p][:, g, 0:1].to_broadcast([P, P]), ident[:])
                last.then_inc(mm["att_rows"], 1)

            pe.wait_ge(const_made, 3)
            pe.wait_ge(w_lo, W_OF_PHASE["A"][1])
            run(pe, {
                "adj_norm": turn_rows("adj_norm", adj_n, "adj_n"),
                "turn0": turn("turn0", 0),
                "sage_y": project("sage_y", hT_a, read["turn0"], w_agg, feat),
                "sage": project_and_spread("sage", hT_a, read["turn0"], w_self, adjT_n, sage_y,
                                           [read["adj_norm"], read["sage_y"]]),
                "turn1": turn("turn1", 1),
                "qk": project("qk", hT_a, read["turn1"], w_qk, 2 * att),
                "adj_k": spread("adj_k", adjT_a, key, att, [read["qk"], got["adjT_a"]]),
                "logit_row": logit_row,
                "value": project("value", hT_a, read["turn1"], w_val, feat),
                "prob_col": prob_column,
                "turn2": turn("turn2", 2),
                "sup1": project("sup1", hT_b, read["turn2"], w_gcn[0], feat),
                "hid1": spread_hidden("hid1", read["sup1"]),
                "sup2": project_hidden("sup2", got["hid1_half"], w_gcn[1]),
                "hid2": spread_hidden("hid2", read["sup2"]),
                "sup3": project_hidden("sup3", got["hid2_half"], w_gcn[2]),
                "gcn": spread("gcn", adjT_b, sup, feat, [read["sup3"]]),
                "turn3": turn("turn3", 3),
                "att_cols": project("att_cols", hT_c, read["turn3"], w_att, 2),
                "diff_y": project("diff_y", hT_c, read["turn3"], w_hop[2], feat),
                "att_rows": att_rows,
                "trans": turn_rows("trans", trans, "trans"),
                "diff_z": project_and_spread("diff_z", hT_c, read["turn3"], w_hop[1], transT, diff,
                                             [read["trans"], read["diff_y"]]),
                "diffuse": project_and_spread("diffuse", hT_c, read["turn3"], w_hop[0], transT, diff,
                                              [read["diff_z"]]),
            }, ORDER, lambda t: pe.wait_ge(w_lo, (W_OF_PHASE["B"][1], W_ATT)[t]) if t < 2 else None)


_OUT = (128, 128, 256)


def kernel(**inputs):
    import numpy as _np
    import concourse.bacc as _bacc
    from concourse import mybir as _mybir
    from concourse.bass_utils import run_bass_kernel_spmd as _run

    given = {name: _np.asarray(a) for name, a in inputs.items()}
    laid_out = [
        ("x", given["x"]), ("adj", given["adj"]), ("adj_t", given["adj"].transpose(0, 2, 1)),
        ("w0_t", given["L0_gnn_W"].T), ("wqk_t", given["L1_gnn_W_qk"].T), ("wv_t", given["L1_gnn_W_v"].T),
        ("w1", given["L2_gnn_W1"]), ("w2", given["L2_gnn_W2"]), ("w3", given["L2_gnn_W3"]),
        ("b12", _np.stack([given["L2_gnn_b1"], given["L2_gnn_b2"]]).reshape(2, 2, 128).transpose(2, 0, 1)),
        ("b3", given["L2_gnn_b3"]),
        ("att_w", given["L3_gnn_Wv"]), ("att_b", given["L3_gnn_bv"]), ("att_vec", given["L3_gnn_aw"]),
        ("att_c", given["L3_gnn_ab"]), ("wk", given["L3_gnn_Wk"]), ("bk", given["L3_gnn_bk"]),
    ]
    nc = _bacc.Bacc("TRN2", target_bir_lowering=False, num_devices=1)
    arrays, args = {}, []
    for name, a in laid_out:
        a = _np.ascontiguousarray(a)
        arrays[f"in_{name}_dram"] = a
        args.append(nc.dram_tensor(f"in_{name}_dram", a.shape, _mybir.dt.from_np(a.dtype), kind="ExternalInput").ap())
    args.append(nc.dram_tensor("out_dram", _OUT, _mybir.dt.float32, kind="ExternalOutput").ap())
    build(nc, *args)
    r = _run(nc, [arrays], core_ids=[0])
    return r.results[0]["out_dram"]
```

```python
from contextlib import ExitStack

import concourse.bass as bass
from concourse import mybir

F32 = mybir.dt.float32
F32R = mybir.dt.float32r
ALU = mybir.AluOpType
ACT = mybir.ActivationFunctionType
AX_X = mybir.AxisListType.X

P = 128
BANKS = 8
LAYERNORM_EPS = 1e-5
DEGREE_EPS = 1e-6
ROW_SUM_EPS = 1e-12
LEAKY_SLOPE = 0.2
SMALL_LOADS = 7

PAIR_EVERY = 19.3
TENSOR = {
    "turn0": 3.51, "adj_norm": 3.80, "sage_y": 5.60, "sage": 7.04, "turn1": 12.71, "qkv0": 18.59,
    "qkv1": 19.11, "adj_k": 20.74, "logit_row": 23.26, "prob_col": 26.00, "turn2": 33.97, "sup1": 35.85,
    "hid1": 38.93, "sup2": 43.13, "hid2": 46.68, "sup3": 53.64, "gcn": 56.68, "turn3": 66.44,
    "diff_y0": 69.42, "diff_y1": 70.09, "att_rows": 73.94, "trans": 81.34, "diff_z": 85.98, "diffuse": 98.13,
}
SCALAR = {
    "adj_n": 3.08, "adj_norm": 4.22, "turn0": 4.36, "sage_y": 7.10, "turn1": 13.35, "qkv0": 19.77,
    "qkv1": 20.29, "softmax": 25.12, "turn2": 34.61, "adj_hi": 36.15, "sup1": 37.35, "hid1": 40.30,
    "hid1_hi": 41.24, "sup2": 44.63, "hid2": 47.75, "hid2_hi": 50.89, "sup3": 55.14, "turn3": 67.43,
    "diff_y0": 70.47, "diff_y1": 71.06, "att_rows": 74.96, "exponent": 78.44, "transition": 80.62,
    "trans": 81.86, "diff_z": 93.05,
}
VECTOR = {
    "degree": 0.00, "stats0": 0.18, "moments0": 1.27, "degree_inv": 2.21, "scale0": 2.79, "adj_norm": 4.56,
    "turn0": 4.93, "sage_y": 7.67, "sage": 9.21, "stats1": 9.88, "moments1": 10.77, "scale1": 11.99,
    "turn1": 17.92, "adj_k": 22.90, "logit_row": 24.55, "quotient": 25.53, "prob_col": 26.72, "attend": 27.29,
    "stats2": 29.54, "moments2": 31.03, "scale2": 33.25, "turn2": 35.18, "sup3": 55.71, "gcn": 57.53,
    "stats3": 60.27, "moments3": 61.16, "scale3": 64.34, "turn3": 68.75, "diff_y0": 72.81, "diff_y1": 73.34,
    "leaky": 77.93, "alpha": 78.92, "row_inv": 79.92, "trans": 82.80, "diff_z": 93.62, "diffuse": 100.30,
}
GPSIMD = {
    "rstd0": 1.79, "rstd1": 10.99, "rstd2": 32.25, "x2_bias": 35.85, "adj_lo": 38.52, "hid1_lo": 41.83,
    "hid2_lo": 52.04, "rstd3": 61.78, "x3_bias": 75.10, "y": 100.97,
}
SYNC = {
    "x0": VECTOR["sage"] - 2 * PAIR_EVERY, "adj_a": SCALAR["adj_n"] - 2 * PAIR_EVERY,
    "adjT_a": TENSOR["adj_k"] - 2 * PAIR_EVERY, "adjT_b": TENSOR["gcn"] - 2 * PAIR_EVERY,
    "adj_c": VECTOR["alpha"] - 2 * PAIR_EVERY, "store": GPSIMD["y"],
}


def in_order(places):
    cycle = 2 * PAIR_EVERY
    at = [(t + p * PAIR_EVERY, step, p) for step, t in places.items() for p in range(2)]
    first = min(int(t // cycle) for t, _, _ in at)
    return [(step, p, int(t // cycle) - first) for _, t, step, p in sorted((t % cycle, t, step, p) for t, step, p in at)]


def build(nc, x, adj, adj_t, w0_t, wqk_t, wv_t, w1, w2, w3, b12, b3, att_w, att_b, att_vec, att_c, wk, bk, out):
    graphs, nodes, feat = x.shape
    att = wqk_t.shape[1] // 2
    hops = wk.shape[0]
    pairs = graphs // 2
    groups = pairs // 2
    assert nodes == P and feat == 2 * P and hops == 3
    fc = feat // P

    x_d = x.rearrange("(j g) n d -> j n g d", g=2)
    adj_d = adj.rearrange("(j g) n m -> j n g m", g=2)
    adj_t_d = adj_t.rearrange("(j g) m n -> j m g n", g=2)
    out_d = out.rearrange("(j g) n d -> j n g d", g=2)

    with ExitStack() as ctx:
        def sb(name, shape, dt=F32):
            return ctx.enter_context(nc.sbuf_tensor(name, shape, dt))

        def pair_buf(name, shape, dt=F32):
            return [sb(f"{name}_p{p}", shape, dt) for p in range(2)]

        def split_buf(name, shape):
            return [(sb(f"{name}_hi_p{p}", shape, F32R), sb(f"{name}_lo_p{p}", shape, F32R)) for p in range(2)]

        def weight(name, cols):
            return sb(f"{name}_hi", [P, fc, cols], F32R), sb(f"{name}_lo", [P, fc, cols], F32R)

        w_self, w_agg = weight("w_self", feat), weight("w_agg", feat)
        w_qkv = weight("w_qkv", 2 * att + feat)
        w_gcn = [weight(f"w_gcn{i}", feat) for i in range(3)]
        w_hop = [weight(f"w_hop{i}", feat + 2 * (i == hops - 1)) for i in range(hops)]
        ident = sb("ident", [P, P])
        minus_half = sb("minus_half", [P, 2])
        bias_hid = sb("bias_hid", [P, 2, fc])
        bias_gcn = sb("bias_gcn", [P, feat])
        bias_hops = sb("bias_hops", [P, hops, feat])
        bias_diff = sb("bias_diff", [P, feat])
        minus_bias_diff = sb("minus_bias_diff", [P, feat])
        att_bias = sb("att_bias", [P, 4])
        att_stage = sb("att_stage", [P, fc, feat])
        att_rows_w = sb("att_rows_w", [P, 2, feat])
        att_b_row = sb("att_b_row", [P, feat])
        att_cols_w = sb("att_cols_w", [P, fc, 2])

        x0 = pair_buf("x0", [P, 2, feat])
        x1 = pair_buf("x1", [P, 2, feat])
        x2 = pair_buf("x2", [P, 2, feat])
        x3 = pair_buf("x3", [P, 2, feat])
        x2_bias = pair_buf("x2_bias", [P, 2, feat])
        x3_bias = pair_buf("x3_bias", [P, 2, feat])
        floored = pair_buf("floored", [P, 2, feat])
        y = pair_buf("y", [P, 2, feat])
        stats = [pair_buf(f"stats{l}", [P, 2, 6]) for l in range(4)]
        mean_var = [pair_buf(f"mean_var{l}", [P, 2, 2]) for l in range(4)]
        var_eps = [pair_buf(f"var_eps{l}", [P, 2]) for l in range(4)]
        rstd = [pair_buf(f"rstd{l}", [P, 2]) for l in range(4)]
        z = [pair_buf(f"z{l}", [P, 2, feat]) for l in range(4)]
        hT_a = split_buf("hT_a", [P, 2, fc, P])
        hT_b = split_buf("hT_b", [P, 2, fc, P])
        hT_c = split_buf("hT_c", [P, 2, fc, P])
        adj_a = pair_buf("adj_a", [P, 2, P])
        adj_c = pair_buf("adj_c", [P, 2, P])
        adjT_a = pair_buf("adjT_a", [P, 2, P])
        adjT_b_in = pair_buf("adjT_b_in", [P, 2, P])
        adjT_b = split_buf("adjT_b", [P, 2, P])
        deg = pair_buf("deg", [P, 2])
        deg_floor = pair_buf("deg_floor", [P, 2])
        deg_inv = pair_buf("deg_inv", [P, 2])
        adj_n = pair_buf("adj_n", [P, 2, P])
        adjT_n = split_buf("adjT_n", [P, 2, P])
        sage_y = split_buf("sage_y", [P, 2, feat])
        qkv = pair_buf("qkv", [P, 2, 2 * att + feat])
        qk_prod = pair_buf("qk_prod", [P, 2, att])
        logit = pair_buf("logit", [P, 2])
        logit_max = pair_buf("logit_max", [2, 1])
        exp_bias = pair_buf("exp_bias", [2, 1])
        prob = pair_buf("prob", [2, P])
        prob_sum = pair_buf("prob_sum", [2, 1])
        prob_inv = pair_buf("prob_inv", [2, 1])
        prob_n = pair_buf("prob_n", [2, P])
        prob_col = pair_buf("prob_col", [P, 2])
        sup_whole = pair_buf("sup_whole", [P, 2, feat])
        sup = split_buf("sup", [P, 2, feat])
        hid = pair_buf("hid", [P, fc, 2, P])
        hidT = split_buf("hidT", [P, fc, 2, P])
        att_col = pair_buf("att_col", [P, 2, 2])
        pair_score = pair_buf("pair_score", [P, 2, P])
        leaky = pair_buf("leaky", [P, 2, P])
        expo = pair_buf("expo", [P, 2, P])
        alpha = pair_buf("alpha", [P, 2, P])
        row_sum = pair_buf("row_sum", [P, 2])
        row_inv = pair_buf("row_inv", [P, 2])
        trans = pair_buf("trans", [P, 2, P])
        transT = split_buf("transT", [P, 2, P])
        diff = split_buf("diff", [P, 2, feat])

        stage = [*x2_bias, *z[2], *y, *x3_bias, *z[3]]

        bank = [ctx.enter_context(nc.psum_tensor(f"bank{i}", [P, 512], F32)) for i in range(BANKS)]

        def sem(name):
            return ctx.enter_context(nc.semaphore(name))

        def each(names):
            return {name: sem(name) for name in names.split()}

        mm = {step: sem(f"{step}_mm") for step in TENSOR}
        hi = {s: sem(f"{s}_hi") for s in
              "adj_norm turn0 sage_y turn1 turn2 hid1 hid2 sup3 turn3 diff_y0 diff_y1 trans diff_z".split()}
        read = {s: sem(f"{s}_read") for s in mm}
        got = each("stats0 stats1 stats2 stats3 moments0 moments1 moments2 moments3 var_eps0 var_eps1 var_eps2 "
                   "var_eps3 rstd0 rstd1 rstd2 rstd3 z0 z1 z2 z3 deg deg_floor deg_inv adj_n x2 "
                   "adjT_b_hi adjT_b logit_max exp_bias prob prob_inv prob_n x2_bias x3_bias att_cols "
                   "hid1_split hid2_split leaky expo alpha row_inv trans y")
        landed = {name: [sem(f"{name}_landed_p{p}") for p in range(2)]
                  for name in "x0 adj_a adjT_a adjT_b adj_c out".split()}
        w_landed = [sem(f"w_landed{i}") for i in range(10)]
        small_landed = sem("small_landed")
        w_hi, w_lo = sem("w_hi"), sem("w_lo")
        const_made = sem("const_made")
        att_made = sem("att_made")
        bias_made = sem("bias_made")

        def active(t, lag):
            return not isinstance(t, int) or 0 <= t - lag < groups

        def run(eng, order, steps):
            def turn(t):
                for step, p, lag in order:
                    if active(t, lag):
                        steps[step](t, (t - lag) * 2 + (p + 1), p)

            last = max(lag for _, _, lag in order)
            for t in range(last + 1):
                turn(t)
            with eng.Fori(last + 1, groups) as t:
                turn(t)
            for t in range(groups, groups + last):
                turn(t)

        def before(n):
            return None if isinstance(n, int) and n <= 2 else n - 2

        def landed_count(n, p):
            return (n + (1 - p)) // 2 * 16 if isinstance(n, int) else (n + (1 - p)) * 8

        block = ctx.enter_context(nc.Block())

        def part(halves, a, b):
            return tuple(h[:, :, a:b] for h in halves)

        w_att = part(w_hop[hops - 1], feat, feat + 2)

        w_sources = [
            (w0_t[feat:2 * feat, :], w_agg), (w0_t[0:feat, :], w_self), (wqk_t, part(w_qkv, 0, 2 * att)),
            (wv_t, part(w_qkv, 2 * att, 2 * att + feat)), (w1, w_gcn[0]), (w2, w_gcn[1]), (w3, w_gcn[2]),
            (wk[2], part(w_hop[2], 0, feat)), (wk[1], w_hop[1]), (wk[0], w_hop[0]),
        ]
        W_OF_PHASE = {"A": (0, 4), "B": (4, 7), "C": (7, 10)}
        W_ATT = 11
        LATER_WEIGHTS = {"turn0": "B", "turn1": "C"}

        @block.sync
        def _(sp):
            def load(name, dst, src, reader):
                def do(t, n, p):
                    if before(n) is not None:
                        sp.wait_ge(reader, before(n))
                    sp.dma_start(dst[p][:], src[n - 1]).then_inc(landed[name][p], 16)
                return do

            def store(t, n, p):
                sp.wait_ge(got["y"], n)
                sp.dma_start(out_d[n - 1], y[p][:]).then_inc(landed["out"][p], 16)

            def weights(i):
                src, (half, _) = w_sources[i]
                cols = half.shape[2]
                sp.dma_start(stage[i][:, :, 0:cols], src.rearrange("(c p) o -> p c o", p=P)).then_inc(w_landed[i], 16)

            def small(dst, src):
                sp.dma_start(dst, src).then_inc(small_landed, 16)

            loads = {
                "x0": load("x0", x0, x_d, read["sage"]),
                "adj_a": load("adj_a", adj_a, adj_d, got["adj_n"]),
                "adjT_a": load("adjT_a", adjT_a, adj_t_d, mm["adj_k"]),
                "adjT_b": load("adjT_b", adjT_b_in, adj_t_d, mm["gcn"]),
                "adj_c": load("adj_c", adj_c, adj_d, got["alpha"]),
            }
            loads["x0"](0, 1, 0)
            loads["adj_a"](0, 1, 0)
            weights(0)
            weights(1)
            loads["x0"](0, 2, 1)
            loads["adj_a"](0, 2, 1)
            for name in ("adjT_a", "adjT_b", "adj_c"):
                for p in range(2):
                    loads[name](0, p + 1, p)
            for i in range(2, len(w_sources)):
                weights(i)
            small(bias_hid[:], b12)
            small(bias_gcn[:], b3.partition_broadcast(P))
            small(bias_hops[:], bk.partition_broadcast(P))
            small(att_stage[:], att_w.rearrange("(c p) o -> p c o", p=P))
            small(att_rows_w[:], att_vec.rearrange("(s d) o -> (o s) d", s=2).partition_broadcast(P))
            small(att_b_row[:], att_b.partition_broadcast(P))
            small(att_bias[:, 0:1], att_c.partition_broadcast(P))

            def next_load(do):
                def later(t, n, p):
                    if not isinstance(n, int) or n > 2:
                        do(t, n, p)
                return later

            run(sp, in_order(SYNC), {"store": store} | {name: next_load(do) for name, do in loads.items()})
            for p in range(2):
                sp.wait_ge(landed["out"][p], 16 * groups)

        @block.gpsimd
        def _(pool):
            nc.gpsimd.memset(ident[:], 0.0).then_inc(const_made, 1)
            pool.wait_ge(const_made, 1)
            nc.gpsimd.affine_select(out=ident[:], in_=ident[:], compare_op=ALU.not_equal, fill=1.0, base=0,
                                    pattern=[[-1, P]], channel_multiplier=1).then_inc(const_made, 1)
            nc.gpsimd.memset(minus_half[:], -0.5).then_inc(const_made, 1)
            pool.wait_ge(const_made, 3)

            def inverse_deviation(l):
                def do(t, n, p):
                    pool.wait_ge(got[f"moments{l}"], n)
                    pool.nop(nofuse=True)
                    nc.gpsimd.tensor_scalar(var_eps[l][p][:], mean_var[l][p][:, :, 1], LAYERNORM_EPS, None,
                                            ALU.add).then_inc(got[f"var_eps{l}"], 1)
                    pool.wait_ge(got[f"var_eps{l}"], n)
                    nc.gpsimd.tensor_tensor(rstd[l][p][:], var_eps[l][p][:], minus_half[:],
                                            ALU.pow).then_inc(got[f"rstd{l}"], 1)
                return do

            def x2_plus_bias(t, n, p):
                pool.wait_ge(got["x2"], n)
                if before(n) is not None:
                    pool.wait_ge(read["gcn"], before(n))
                if isinstance(n, int) and n == 1:
                    pool.wait_ge(small_landed, 16 * SMALL_LOADS)
                nc.gpsimd.tensor_tensor(x2_bias[p][:], x2[p][:], bias_gcn[:].unsqueeze(1).to_broadcast([P, 2, feat]),
                                        ALU.add).then_inc(got["x2_bias"], 1)

            def adj_lo(t, n, p):
                pool.wait_ge(got["adjT_b_hi"], n)
                h, l = adjT_b[p]
                nc.gpsimd.tensor_tensor(l[:], adjT_b_in[p][:], h[:].bitcast(F32), ALU.subtract).then_inc(got["adjT_b"], 1)

            def hidden_lo(step):
                def do(t, n, p):
                    pool.wait_ge(hi[step], n)
                    h, l = hidT[p]
                    nc.gpsimd.tensor_tensor(l[:], hid[p][:], h[:].bitcast(F32),
                                            ALU.subtract).then_inc(got[f"{step}_split"], 1)
                return do

            def x3_plus_bias(t, n, p):
                pool.wait_ge(read["gcn"], n)
                if isinstance(n, int) and n == 1:
                    pool.wait_ge(bias_made, hops)
                if before(n) is not None:
                    pool.wait_ge(got["y"], before(n))
                nc.gpsimd.tensor_tensor(x3_bias[p][:], x3[p][:], bias_diff[:].unsqueeze(1).to_broadcast([P, 2, feat]),
                                        ALU.add).then_inc(got["x3_bias"], 1)

            def finish(t, n, p):
                pool.wait_ge(got["x3_bias"], n)
                if before(n) is not None:
                    pool.wait_ge(landed["out"][p], landed_count(n, p) - 16)
                pool.wait_ge(read["diffuse"], n)
                nc.gpsimd.tensor_tensor(y[p][:], floored[p][:], x3_bias[p][:], ALU.add).then_inc(got["y"], 1)

            run(pool, in_order(GPSIMD), {
                "rstd0": inverse_deviation(0), "rstd1": inverse_deviation(1), "rstd2": inverse_deviation(2),
                "rstd3": inverse_deviation(3), "x2_bias": x2_plus_bias, "adj_lo": adj_lo,
                "hid1_lo": hidden_lo("hid1"), "hid2_lo": hidden_lo("hid2"), "x3_bias": x3_plus_bias, "y": finish,
            })

        tensor_order = in_order(TENSOR)
        bank_of = {(step, p): bank[i % BANKS] for i, (step, p, _) in enumerate(tensor_order)}
        assert len(tensor_order) % BANKS == 0

        def view(step, p, *dims):
            size = 1
            for d in dims:
                size *= d
            b = bank_of[step, p][:, 0:size]
            if len(dims) == 2:
                return b.rearrange("p (a b) -> p a b", b=dims[1])
            if len(dims) == 3:
                return b.rearrange("p (a b c) -> p a b c", b=dims[1], c=dims[2])
            return b

        @block.scalar
        def _(act):
            def weights(phase):
                for i in range(*W_OF_PHASE[phase]):
                    half = w_sources[i][1][0]
                    act.wait_ge(w_landed[i], 16)
                    nc.scalar.activation(half[:, :, :], stage[i][:, :, 0:half.shape[2]], ACT.Copy).then_inc(w_hi, 1)
                if phase == "C":
                    act.wait_ge(att_made, 4)
                    nc.scalar.activation(w_att[0], att_cols_w[:], ACT.Copy).then_inc(w_hi, 1)

            def take_hi(step, halves, func, *dims):
                def do(t, n, p):
                    act.wait_ge(mm[step], n)
                    nc.scalar.activation(halves[p][0][:], view(step, p, *dims), func).then_inc(hi[step], 1)
                    if isinstance(n, int) and n == 1 and step in LATER_WEIGHTS:
                        weights(LATER_WEIGHTS[step])
                return do

            def adj_rows(t, n, p):
                act.wait_ge(got["deg_inv"], n)
                if before(n) is not None:
                    act.wait_ge(mm["adj_norm"], before(n))
                for g in range(2):
                    last = nc.scalar.activation(adj_n[p][:, g, :], adj_a[p][:, g, :], ACT.Copy,
                                                scale=deg_inv[p][:, g:g + 1])
                last.then_inc(got["adj_n"], 1)

            def transition(t, n, p):
                act.wait_ge(got["row_inv"], n)
                if before(n) is not None:
                    act.wait_ge(mm["trans"], before(n))
                for g in range(2):
                    last = nc.scalar.activation(trans[p][:, g, :], alpha[p][:, g, :], ACT.Copy,
                                                scale=row_inv[p][:, g:g + 1])
                last.then_inc(got["trans"], 1)

            def take_whole(step):
                def do(t, n, p):
                    act.wait_ge(mm[step], n)
                    nc.scalar.activation(sup_whole[p][:], view(step, p, 2, feat), ACT.Copy).then_inc(read[step], 1)
                return do

            def take_qkv(step, g):
                def do(t, n, p):
                    act.wait_ge(mm[step], n)
                    if before(n) is not None:
                        act.wait_ge(got["x2"], before(n))
                    nc.scalar.activation(qkv[p][:, g, :], view(step, p, 2 * att + feat), ACT.Copy).then_inc(read[step], 1)
                return do

            def take_hi_graph(step, g):
                def do(t, n, p):
                    act.wait_ge(mm[step], n)
                    nc.scalar.activation(diff[p][0][:, g, :], view(step, p, feat), ACT.Copy).then_inc(hi[step], 1)
                return do

            def adj_hi(t, n, p):
                act.wait_ge(landed["adjT_b"][p], landed_count(n, p))
                nc.scalar.activation(adjT_b[p][0][:], adjT_b_in[p][:], ACT.Copy).then_inc(got["adjT_b_hi"], 1)

            def softmax(t, n, p):
                act.wait_ge(got["exp_bias"], n)
                if before(n) is not None:
                    act.wait_ge(got["prob_n"], before(n))
                nc.scalar.activation(prob[p][:], view("logit_row", p, P)[0:2, :], ACT.Exp, bias=exp_bias[p][:, 0:1],
                                     scale=float(att) ** -0.5, accum_out=prob_sum[p][:, 0:1]).then_inc(got["prob"], 1)

            def hidden(step, layer):
                def do(t, n, p):
                    act.wait_ge(mm[step], n)
                    if step == "hid2":
                        act.wait_ge(got["hid1_split"], n)
                    elif before(n) is not None:
                        act.wait_ge(got["hid2_split"], before(n))
                    v = view(step, p, fc, 2, P)
                    for c in range(fc):
                        last = nc.scalar.activation(hid[p][:, c], v[:, c], ACT.Relu,
                                                    bias=bias_hid[:, layer, c:c + 1])
                    last.then_inc(read[step], 1)
                return do

            def hidden_hi(step):
                def do(t, n, p):
                    act.wait_ge(read[step], n)
                    nc.scalar.activation(hidT[p][0][:], hid[p][:], ACT.Copy).then_inc(hi[step], 1)
                return do

            def att_rows(t, n, p):
                act.wait_ge(mm["att_rows"], n)
                v = view("att_rows", p, 2, P)
                if before(n) is not None:
                    act.wait_ge(got["leaky"], before(n))
                for g in range(2):
                    last = nc.scalar.activation(pair_score[p][:, g, :], v[:, g, :], ACT.Identity,
                                                bias=att_col[p][:, g, 1:2])
                last.then_inc(read["att_rows"], 1)

            def exponent(t, n, p):
                act.wait_ge(got["leaky"], n)
                if before(n) is not None:
                    act.wait_ge(got["alpha"], before(n))
                nc.scalar.activation(expo[p][:], leaky[p][:], ACT.Exp).then_inc(got["expo"], 1)

            weights("A")
            act.wait_ge(small_landed, 16 * SMALL_LOADS)
            run(act, in_order(SCALAR), {
                "adj_n": adj_rows, "adj_norm": take_hi("adj_norm", adjT_n, ACT.Copy, 2, P),
                "turn0": take_hi("turn0", hT_a, ACT.Relu, 2, fc, P),
                "sage_y": take_hi("sage_y", sage_y, ACT.Copy, 2, feat),
                "turn1": take_hi("turn1", hT_a, ACT.Relu, 2, fc, P),
                "qkv0": take_qkv("qkv0", 0), "qkv1": take_qkv("qkv1", 1), "softmax": softmax,
                "adj_hi": adj_hi, "turn2": take_hi("turn2", hT_b, ACT.Relu, 2, fc, P),
                "sup1": take_whole("sup1"), "hid1": hidden("hid1", 0), "hid1_hi": hidden_hi("hid1"),
                "sup2": take_whole("sup2"), "hid2": hidden("hid2", 1), "hid2_hi": hidden_hi("hid2"),
                "sup3": take_hi("sup3", sup, ACT.Copy, 2, feat),
                "turn3": take_hi("turn3", hT_c, ACT.Relu, 2, fc, P),
                "diff_y0": take_hi_graph("diff_y0", 0), "diff_y1": take_hi_graph("diff_y1", 1),
                "att_rows": att_rows, "exponent": exponent, "transition": transition,
                "trans": take_hi("trans", transT, ACT.Copy, 2, P),
                "diff_z": take_hi("diff_z", diff, ACT.Copy, 2, feat),
            })

        @block.vector
        def _(dve):
            def weights(phase):
                for i in range(*W_OF_PHASE[phase]):
                    h, l = w_sources[i][1]
                    dve.wait_ge(w_hi, i + 1)
                    nc.vector.tensor_tensor(l[:, :, :], stage[i][:, :, 0:h.shape[2]], h[:, :, :].bitcast(F32),
                                            ALU.subtract).then_inc(w_lo, 1)
                if phase == "B":
                    attention_weights()
                    for i in range(1, hops):
                        other = bias_hops[:, 0, :] if i == 1 else bias_diff[:]
                        if i > 1:
                            dve.wait_ge(bias_made, i - 1)
                        nc.vector.tensor_tensor(bias_diff[:], other, bias_hops[:, i, :],
                                                ALU.add).then_inc(bias_made, 1)
                    dve.wait_ge(bias_made, hops - 1)
                    nc.vector.tensor_scalar(minus_bias_diff[:], bias_diff[:], -1.0, None,
                                            ALU.mult).then_inc(bias_made, 1)
                if phase == "C":
                    dve.wait_ge(w_hi, W_ATT)
                    nc.vector.tensor_tensor(w_att[1], att_cols_w[:], w_att[0].bitcast(F32),
                                            ALU.subtract).then_inc(w_lo, 1)

            def attention_weights():
                junk = leaky[0][:].rearrange("p g m -> p (g m)")
                dve.wait_ge(small_landed, 16 * SMALL_LOADS)
                for c in range(fc):
                    for s in range(2):
                        nc.vector.tensor_tensor_reduce(junk, att_stage[:, c, :], att_rows_w[:, s, :], 1.0,
                                                       0.0, ALU.mult, ALU.add,
                                                       att_cols_w[:, c, s:s + 1]).then_inc(att_made, 1)
                        dve.wait_ge(att_made, fc * c + s + 1)
                for s in range(2):
                    nc.vector.tensor_tensor_reduce(junk, att_b_row[:], att_rows_w[:, s, :], 1.0, 0.0,
                                                   ALU.mult, ALU.add, att_bias[:, s + 1:s + 2]).then_inc(att_made, 1)
                    dve.wait_ge(att_made, 2 * fc + s + 1)
                nc.vector.reduce_sum(att_bias[:, 3:4], att_bias[:, 0:3], AX_X).then_inc(att_made, 1)

            def layer_stats(l, src, ready):
                def do(t, n, p):
                    if l == 0:
                        dve.wait_ge(landed["x0"][p], landed_count(n, p))
                    else:
                        dve.wait_ge(ready, n)
                    for g in range(2):
                        last = nc.vector.bn_stats(stats[l][p][:, g, :], src[p][:, g, :])
                    last.then_inc(got[f"stats{l}"], 1)
                return do

            def moments(l):
                def do(t, n, p):
                    dve.wait_ge(got[f"stats{l}"], n)
                    dve.nop(nofuse=True)
                    if before(n) is not None:
                        dve.wait_ge(got[f"z{l}"], before(n))
                        dve.nop(nofuse=True)
                    for g in range(2):
                        last = nc.vector.bn_aggr(mean_var[l][p][:, g, :], stats[l][p][:, g, :])
                    last.then_inc(got[f"moments{l}"], 1)
                return do

            def scale(l, src):
                def do(t, n, p):
                    dve.wait_ge(got[f"rstd{l}"], n)
                    if before(n) is not None:
                        dve.wait_ge(mm[f"turn{l}"], before(n))
                    for g in range(2):
                        last = nc.vector.tensor_scalar(z[l][p][:, g, :], src[p][:, g, :], mean_var[l][p][:, g, 0:1],
                                                       rstd[l][p][:, g:g + 1], ALU.subtract, ALU.mult)
                    last.then_inc(got[f"z{l}"], 1)
                return do

            def degree(t, n, p):
                dve.wait_ge(landed["adj_a"][p], landed_count(n, p))
                nc.vector.reduce_sum(deg[p][:], adj_a[p][:], AX_X).then_inc(got["deg"], 1)

            def degree_inverse(t, n, p):
                dve.wait_ge(got["deg"], n)
                nc.vector.tensor_scalar(deg_floor[p][:], deg[p][:], DEGREE_EPS, None,
                                        ALU.max).then_inc(got["deg_floor"], 1)
                dve.wait_ge(got["deg_floor"], n)
                if before(n) is not None:
                    dve.wait_ge(got["adj_n"], before(n))
                nc.vector.reciprocal(deg_inv[p][:], deg_floor[p][:]).then_inc(got["deg_inv"], 1)

            def take_lo(step, halves, *dims):
                def do(t, n, p):
                    h, l = halves[p]
                    dve.wait_ge(hi[step], n)
                    nc.vector.tensor_tensor(l[:], view(step, p, *dims), h[:].bitcast(F32),
                                            ALU.subtract).then_inc(read[step], 1)
                return do

            def take_relu_lo(step, halves):
                def do(t, n, p):
                    h, l = halves[p]
                    dve.wait_ge(hi[step], n)
                    b = bank_of[step, p][:]
                    nc.vector.scalar_tensor_tensor(l[:].rearrange("p a b c -> p (a b c)"), b, 0.0,
                                                   h[:].bitcast(F32).rearrange("p a b c -> p (a b c)"), ALU.max,
                                                   ALU.subtract).then_inc(read[step], 1)
                    if isinstance(n, int) and n == 1 and step in LATER_WEIGHTS:
                        weights(LATER_WEIGHTS[step])
                return do

            def sage(t, n, p):
                dve.wait_ge(mm["sage"], n)
                nc.vector.scalar_tensor_tensor(x1[p][:], view("sage", p, 2, feat), 0.0, x0[p][:], ALU.max,
                                               ALU.add).then_inc(read["sage"], 1)

            def adj_k(t, n, p):
                dve.wait_ge(mm["adj_k"], n)
                if before(n) is not None:
                    dve.wait_ge(mm["logit_row"], before(n))
                v = view("adj_k", p, 2, att)
                for g in range(2):
                    last = nc.vector.tensor_tensor_reduce(qk_prod[p][:, g, :], v[:, g, :], qkv[p][:, g, 0:att], 1.0, 0.0,
                                                          ALU.mult, ALU.add, logit[p][:, g:g + 1])
                last.then_inc(read["adj_k"], 1)

            def logit_row(t, n, p):
                dve.wait_ge(mm["logit_row"], n)
                nc.vector.reduce_max(logit_max[p][:], view("logit_row", p, P)[0:2, :],
                                     AX_X).then_inc(got["logit_max"], 1)
                dve.wait_ge(got["logit_max"], n)
                if before(n) is not None:
                    dve.wait_ge(got["prob"], before(n))
                nc.vector.tensor_scalar(exp_bias[p][:], logit_max[p][:], -float(att) ** -0.5, None,
                                        ALU.mult).then_inc(got["exp_bias"], 1)

            def quotient(t, n, p):
                dve.wait_ge(got["prob"], n)
                nc.vector.reciprocal(prob_inv[p][:], prob_sum[p][:]).then_inc(got["prob_inv"], 1)
                dve.wait_ge(got["prob_inv"], n)
                if before(n) is not None:
                    dve.wait_ge(mm["prob_col"], before(n))
                nc.vector.tensor_scalar(prob_n[p][:], prob[p][:], prob_inv[p][:, 0:1], None,
                                        ALU.mult).then_inc(got["prob_n"], 1)

            def prob_column(t, n, p):
                dve.wait_ge(mm["prob_col"], n)
                nc.vector.tensor_copy(prob_col[p][:], view("prob_col", p, 2)).then_inc(read["prob_col"], 1)

            def attend(t, n, p):
                dve.wait_ge(read["prob_col"], n)
                if before(n) is not None:
                    dve.wait_ge(got["x2_bias"], before(n))
                for g in range(2):
                    last = nc.vector.scalar_tensor_tensor(x2[p][:, g, :], qkv[p][:, g, 2 * att:], prob_col[p][:, g:g + 1],
                                                          x1[p][:, g, :], ALU.mult, ALU.add)
                last.then_inc(got["x2"], 1)

            def gcn(t, n, p):
                dve.wait_ge(mm["gcn"], n)
                dve.wait_ge(got["x2_bias"], n)
                if before(n) is not None:
                    dve.wait_ge(got["x3_bias"], before(n))
                nc.vector.tensor_tensor(x3[p][:], view("gcn", p, 2, feat), x2_bias[p][:],
                                        ALU.add).then_inc(read["gcn"], 1)

            def diff_y(step, g):
                def do(t, n, p):
                    dve.wait_ge(hi[step], n)
                    v = view(step, p, feat + 2)
                    if before(n) is not None:
                        dve.wait_ge(read["att_rows"], before(n))
                    nc.vector.tensor_copy(att_col[p][:, g, 0:1], v[:, feat:feat + 1])
                    last = nc.vector.tensor_scalar(att_col[p][:, g, 1:2], v[:, feat + 1:feat + 2], att_bias[:, 3:4],
                                                   None, ALU.add)
                    if g == 1:
                        last.then_inc(got["att_cols"], 1)
                    h, l = diff[p]
                    nc.vector.tensor_tensor(l[:, g, :], v[:, 0:feat], h[:, g, :].bitcast(F32),
                                            ALU.subtract).then_inc(read[step], 1)
                return do

            def leaky_relu(t, n, p):
                dve.wait_ge(read["att_rows"], n)
                if before(n) is not None:
                    dve.wait_ge(got["expo"], before(n))
                s = pair_score[p][:]
                nc.vector.scalar_tensor_tensor(leaky[p][:], s, LEAKY_SLOPE, s, ALU.mult,
                                               ALU.max).then_inc(got["leaky"], 1)

            def alpha_rows(t, n, p):
                dve.wait_ge(landed["adj_c"][p], landed_count(n, p))
                if before(n) is not None:
                    dve.wait_ge(got["trans"], before(n))
                dve.wait_ge(got["expo"], n)
                for g in range(2):
                    last = nc.vector.tensor_tensor_reduce(alpha[p][:, g, :], adj_c[p][:, g, :], expo[p][:, g, :], 1.0,
                                                          ROW_SUM_EPS, ALU.mult, ALU.add, row_sum[p][:, g:g + 1])
                last.then_inc(got["alpha"], 1)

            def row_inverse(t, n, p):
                dve.wait_ge(got["alpha"], n)
                nc.vector.reciprocal(row_inv[p][:], row_sum[p][:]).then_inc(got["row_inv"], 1)

            def diffuse(t, n, p):
                dve.wait_ge(mm["diffuse"], n)
                if before(n) is not None:
                    dve.wait_ge(got["y"], before(n))
                nc.vector.tensor_tensor(floored[p][:], view("diffuse", p, 2, feat),
                                        minus_bias_diff[:].unsqueeze(1).to_broadcast([P, 2, feat]),
                                        ALU.max).then_inc(read["diffuse"], 1)

            weights("A")
            run(dve, in_order(VECTOR), {
                "stats0": layer_stats(0, x0, None), "stats1": layer_stats(1, x1, read["sage"]),
                "stats2": layer_stats(2, x2, got["x2"]), "stats3": layer_stats(3, x3, read["gcn"]),
                "moments0": moments(0), "moments1": moments(1), "moments2": moments(2), "moments3": moments(3),
                "scale0": scale(0, x0), "scale1": scale(1, x1), "scale2": scale(2, x2), "scale3": scale(3, x3),
                "degree": degree, "degree_inv": degree_inverse, "adj_norm": take_lo("adj_norm", adjT_n, 2, P),
                "turn0": take_relu_lo("turn0", hT_a), "turn1": take_relu_lo("turn1", hT_a),
                "turn2": take_relu_lo("turn2", hT_b), "turn3": take_relu_lo("turn3", hT_c),
                "sage_y": take_lo("sage_y", sage_y, 2, feat), "sage": sage, "adj_k": adj_k,
                "logit_row": logit_row, "quotient": quotient, "prob_col": prob_column, "attend": attend,
                "sup3": take_lo("sup3", sup, 2, feat), "gcn": gcn,
                "diff_y0": diff_y("diff_y0", 0), "diff_y1": diff_y("diff_y1", 1),
                "leaky": leaky_relu, "alpha": alpha_rows, "row_inv": row_inverse,
                "trans": take_lo("trans", transT, 2, P), "diff_z": take_lo("diff_z", diff, 2, feat),
                "diffuse": diffuse,
            })

        @block.tensor
        def _(pe):
            place_of = {(step, p): i for i, (step, p, _) in enumerate(tensor_order)}

            def free_bank(t, step, p):
                at, back = place_of[step, p], 0
                while True:
                    at -= BANKS
                    if at < 0:
                        at, back = at + len(tensor_order), back + 1
                    user, q, lag = tensor_order[at]
                    if isinstance(t, int) and t < back:
                        return
                    if active(t - back if isinstance(t, int) else t, lag):
                        break
                user_read = got["prob"] if user == "logit_row" else read[user]
                pe.wait_ge(user_read, (t - back - lag) * 2 + (q + 1))

            def product(out_ap, left, right, start=True, stop=True):
                (lh, ll), (rh, rl) = left, right
                nc.tensor.matmul(out_ap, lh, rl, start=start, stop=False, skip_group_check=True)
                nc.tensor.matmul(out_ap, ll, rh, start=False, stop=False, skip_group_check=True)
                return nc.tensor.matmul(out_ap, lh, rh, start=False, stop=stop, skip_group_check=True)

            def pick(halves, *index):
                return tuple(h[(slice(None), *index)] for h in halves)

            def turn(step, l):
                def do(t, n, p):
                    free_bank(t, step, p)
                    pe.wait_ge(got[f"z{l}"], n)
                    v = view(step, p, 2, fc, P)
                    for g in range(2):
                        for c in range(fc):
                            last = nc.tensor.transpose(v[:, g, c, :], z[l][p][:, g, c * P:(c + 1) * P], ident[:])
                    last.then_inc(mm[step], 1)
                return do

            def turn_rows(step, src, ready):
                def do(t, n, p):
                    free_bank(t, step, p)
                    pe.wait_ge(got[ready], n)
                    v = view(step, p, 2, P)
                    for g in range(2):
                        last = nc.tensor.transpose(v[:, g, :], src[p][:, g, :], ident[:])
                    last.then_inc(mm[step], 1)
                return do

            weights_needed = {"sup1": W_OF_PHASE["B"][1], "diff_y0": W_ATT}

            def first_use(step, n):
                if isinstance(n, int) and n == 1 and step in weights_needed:
                    pe.wait_ge(w_lo, weights_needed[step])

            def project(step, actT, ready, w, cols):
                def do(t, n, p):
                    free_bank(t, step, p)
                    first_use(step, n)
                    pe.wait_ge(ready, n)
                    v = view(step, p, 2, cols)
                    for g in range(2):
                        for c in range(fc):
                            last = product(v[:, g, :], pick(actT[p], g, c), pick(w, c), start=c == 0,
                                           stop=c == fc - 1)
                    last.then_inc(mm[step], 1)
                return do

            def project_graph(step, g, actT, ready, w, cols):
                def do(t, n, p):
                    free_bank(t, step, p)
                    first_use(step, n)
                    pe.wait_ge(ready, n)
                    for c in range(fc):
                        last = product(view(step, p, cols), pick(actT[p], g, c), pick(w, c), start=c == 0,
                                       stop=c == fc - 1)
                    last.then_inc(mm[step], 1)
                return do

            def project_hidden(step, ready, w):
                def do(t, n, p):
                    free_bank(t, step, p)
                    pe.wait_ge(ready, n)
                    v = view(step, p, 2, feat)
                    for g in range(2):
                        for c in range(fc):
                            last = product(v[:, g, :], pick(hidT[p], c, g), pick(w, c), start=c == 0,
                                           stop=c == fc - 1)
                    last.then_inc(mm[step], 1)
                return do

            def project_and_spread(step, actT, ready, w, nodesT, moved, moved_ready):
                def do(t, n, p):
                    free_bank(t, step, p)
                    pe.wait_ge(ready, n)
                    v = view(step, p, 2, feat)
                    for g in range(2):
                        for c in range(fc):
                            product(v[:, g, :], pick(actT[p], g, c), pick(w, c), start=g == 0 and c == 0, stop=False)
                    for r in moved_ready:
                        pe.wait_ge(r, n)
                    for g in range(2):
                        last = product(v[:, g, :], pick(nodesT[p], g), pick(moved[p], g), start=False, stop=True)
                    last.then_inc(mm[step], 1)
                return do

            def spread(step, nodesT, moved, cols, ready):
                def do(t, n, p):
                    free_bank(t, step, p)
                    for r in ready:
                        pe.wait_ge(r, n)
                    v = view(step, p, 2, cols)
                    for g in range(2):
                        last = product(v[:, g, :], pick(nodesT[p], g), pick(moved[p], g))
                    last.then_inc(mm[step], 1)
                return do

            def spread_hidden(step, ready):
                def do(t, n, p):
                    free_bank(t, step, p)
                    pe.wait_ge(ready, n)
                    if step == "hid1":
                        pe.wait_ge(landed["adjT_b"][p], landed_count(n, p))
                    v = view(step, p, fc, 2, P)
                    for g in range(2):
                        for c in range(fc):
                            last = nc.tensor.matmul(v[:, c, g, :], sup_whole[p][:, g, c * P:(c + 1) * P],
                                                    adjT_b_in[p][:, g, :], start=True, stop=True)
                    last.then_inc(mm[step], 1)
                return do

            def adj_k(t, n, p):
                free_bank(t, "adj_k", p)
                pe.wait_ge(read["qkv0"], n)
                pe.wait_ge(read["qkv1"], n)
                pe.wait_ge(landed["adjT_a"][p], landed_count(n, p))
                v = view("adj_k", p, 2, att)
                for g in range(2):
                    last = nc.tensor.matmul(v[:, g, :], adjT_a[p][:, g, :], qkv[p][:, g, att:2 * att], start=True,
                                            stop=True)
                last.then_inc(mm["adj_k"], 1)

            def logit_row(t, n, p):
                free_bank(t, "logit_row", p)
                pe.wait_ge(read["adj_k"], n)
                nc.tensor.matmul(view("logit_row", p, P)[0:2, :], logit[p][:], ident[:], start=True,
                                 stop=True).then_inc(mm["logit_row"], 1)

            def prob_column(t, n, p):
                free_bank(t, "prob_col", p)
                pe.wait_ge(got["prob_n"], n)
                nc.tensor.matmul(view("prob_col", p, 2), prob_n[p][:], ident[0:2, 0:2], start=True,
                                 stop=True).then_inc(mm["prob_col"], 1)

            def att_rows(t, n, p):
                free_bank(t, "att_rows", p)
                pe.wait_ge(got["att_cols"], n)
                v = view("att_rows", p, 2, P)
                for g in range(2):
                    last = nc.tensor.transpose(v[:, g, :], att_col[p][:, g, 0:1].to_broadcast([P, P]), ident[:])
                last.then_inc(mm["att_rows"], 1)

            pe.wait_ge(const_made, 3)
            pe.wait_ge(w_lo, W_OF_PHASE["A"][1])
            run(pe, tensor_order, {
                "adj_norm": turn_rows("adj_norm", adj_n, "adj_n"),
                "turn0": turn("turn0", 0),
                "sage_y": project("sage_y", hT_a, read["turn0"], w_agg, feat),
                "sage": project_and_spread("sage", hT_a, read["turn0"], w_self, adjT_n, sage_y,
                                           [read["adj_norm"], read["sage_y"]]),
                "turn1": turn("turn1", 1),
                "qkv0": project_graph("qkv0", 0, hT_a, read["turn1"], w_qkv, 2 * att + feat),
                "qkv1": project_graph("qkv1", 1, hT_a, read["turn1"], w_qkv, 2 * att + feat),
                "adj_k": adj_k,
                "logit_row": logit_row,
                "prob_col": prob_column,
                "turn2": turn("turn2", 2),
                "sup1": project("sup1", hT_b, read["turn2"], w_gcn[0], feat),
                "hid1": spread_hidden("hid1", read["sup1"]),
                "sup2": project_hidden("sup2", got["hid1_split"], w_gcn[1]),
                "hid2": spread_hidden("hid2", read["sup2"]),
                "sup3": project_hidden("sup3", got["hid2_split"], w_gcn[2]),
                "gcn": spread("gcn", adjT_b, sup, feat, [got["adjT_b"], read["sup3"]]),
                "turn3": turn("turn3", 3),
                "diff_y0": project_graph("diff_y0", 0, hT_c, read["turn3"], w_hop[2], feat + 2),
                "diff_y1": project_graph("diff_y1", 1, hT_c, read["turn3"], w_hop[2], feat + 2),
                "att_rows": att_rows,
                "trans": turn_rows("trans", trans, "trans"),
                "diff_z": project_and_spread("diff_z", hT_c, read["turn3"], w_hop[1], transT, diff,
                                             [read["trans"], read["diff_y0"], read["diff_y1"]]),
                "diffuse": project_and_spread("diffuse", hT_c, read["turn3"], w_hop[0], transT, diff,
                                              [read["diff_z"]]),
            })


_OUT = (128, 128, 256)


def kernel(**inputs):
    import numpy as _np
    import concourse.bacc as _bacc
    from concourse import mybir as _mybir
    from concourse.bass_utils import run_bass_kernel_spmd as _run

    given = {name: _np.asarray(a) for name, a in inputs.items()}
    laid_out = [
        ("x", given["x"]), ("adj", given["adj"]), ("adj_t", given["adj"].transpose(0, 2, 1)),
        ("w0_t", given["L0_gnn_W"].T), ("wqk_t", given["L1_gnn_W_qk"].T), ("wv_t", given["L1_gnn_W_v"].T),
        ("w1", given["L2_gnn_W1"]), ("w2", given["L2_gnn_W2"]), ("w3", given["L2_gnn_W3"]),
        ("b12", _np.stack([given["L2_gnn_b1"], given["L2_gnn_b2"]]).reshape(2, 2, 128).transpose(2, 0, 1)),
        ("b3", given["L2_gnn_b3"]),
        ("att_w", given["L3_gnn_Wv"]), ("att_b", given["L3_gnn_bv"]), ("att_vec", given["L3_gnn_aw"]),
        ("att_c", given["L3_gnn_ab"]), ("wk", given["L3_gnn_Wk"]), ("bk", given["L3_gnn_bk"]),
    ]
    nc = _bacc.Bacc("TRN2", target_bir_lowering=False, num_devices=1)
    arrays, args = {}, []
    for name, a in laid_out:
        a = _np.ascontiguousarray(a)
        arrays[f"in_{name}_dram"] = a
        args.append(nc.dram_tensor(f"in_{name}_dram", a.shape, _mybir.dt.from_np(a.dtype), kind="ExternalInput").ap())
    args.append(nc.dram_tensor("out_dram", _OUT, _mybir.dt.float32, kind="ExternalOutput").ap())
    build(nc, *args)
    r = _run(nc, [arrays], core_ids=[0])
    return r.results[0]["out_dram"]
```

```python
from contextlib import ExitStack

import concourse.bass as bass
from concourse import mybir

F32 = mybir.dt.float32
F32R = mybir.dt.float32r
ALU = mybir.AluOpType
ACT = mybir.ActivationFunctionType
AX_X = mybir.AxisListType.X

P = 128
BANKS = 8
LAYERNORM_EPS = 1e-5
DEGREE_EPS = 1e-6
ROW_SUM_EPS = 1e-12
LEAKY_SLOPE = 0.2
SMALL_LOADS = 7
SCALED_BY_SCALAR = (0, 2, 3)

PAIR_EVERY = 19.45
TENSOR = {
    "turn0": 6.65, "sage_y": 9.41, "sage0": 13.58, "sage1": 13.70, "turn1": 22.58, "qkv1": 25.94,
    "qkv0": 26.46, "adj_k": 28.90, "logit_row": 32.39, "prob_col": 33.49, "near1": 42.11, "hid1": 46.61,
    "near2": 53.78, "hid2": 56.78, "near3": 73.59, "gcn0": 77.09, "gcn1": 80.63, "turn3": 87.46,
    "diff_y0": 94.60, "diff_y1": 94.82, "att_rows": 96.55, "trans": 107.77, "diff_z": 114.61,
    "diffuse": 120.21,
}
SCALAR = {
    "scale0": 5.53, "turn0": 6.28, "adj_hi": 6.40, "sage_y": 9.10, "sage0": 13.27, "sage1": 15.89,
    "turn1": 22.81, "qkv1": 25.79, "qkv0": 26.23, "softmax": 31.94, "scale2": 41.19, "near1": 44.98,
    "hid1": 48.71, "near2": 55.35, "hid2": 61.96, "near3": 76.16, "scale3": 85.74, "turn3": 89.48,
    "diff_y0": 95.91, "diff_y1": 96.58, "att_rows": 99.86, "exponent": 101.65, "transition": 104.01,
    "trans": 111.88, "diff_z": 118.01,
}
VECTOR = {
    "stats0": 1.40, "degree": 2.20, "moments0": 3.15, "degree_inv": 3.57, "turn0": 9.23, "sage_y": 10.76,
    "sage0": 14.98, "sage1": 16.90, "stats1": 17.15, "moments1": 20.50, "scale1": 21.65, "turn1": 25.06,
    "adj_k": 29.82, "logit_row": 33.11, "quotient": 33.83, "prob_col": 34.50, "attend": 34.95,
    "stats2": 35.77, "moments2": 36.52, "near1": 45.63, "hid1": 48.70, "near2": 57.50, "hid2": 62.67,
    "near3": 77.21, "gcn0": 82.84, "gcn1": 83.24, "stats3": 83.42, "moments3": 83.97, "turn3": 92.43,
    "diff_y0": 98.17, "diff_y1": 99.44, "leaky": 102.78, "alpha": 104.88, "row_inv": 105.68, "trans": 113.30,
    "diff_z": 120.63, "diffuse": 126.34,
}
GPSIMD = {
    "rstd0": 0.00, "adj_lo": 4.90, "rstd1": 18.55, "rstd2": 30.57, "x2_bias": 43.54, "rstd3": 81.72,
    "x3_bias": 110.17, "y": 126.84,
}
SYNC = {
    "x0": VECTOR["sage1"] - 2 * PAIR_EVERY, "adj_a": VECTOR["degree"] - 2 * PAIR_EVERY,
    "adjT_a": TENSOR["adj_k"] - 2 * PAIR_EVERY, "adjT_b": TENSOR["near3"] - 2 * PAIR_EVERY,
    "adj_c": VECTOR["alpha"] - 2 * PAIR_EVERY, "store": GPSIMD["y"],
}


def in_order(places):
    cycle = 2 * PAIR_EVERY
    at = [(t + p * PAIR_EVERY, step, p) for step, t in places.items() for p in range(2)]
    first = min(int(t // cycle) for t, _, _ in at)
    return [(step, p, int(t // cycle) - first)
            for _, t, step, p in sorted((t % cycle, t, step, p) for t, step, p in at)]


def build(nc, x, adj, adj_t, w0_t, wqk_t, wv_t, w1, w2, w3, b12, b3, att_w, att_b, att_vec, att_c, wk, bk, out):
    graphs, nodes, feat = x.shape
    att = wqk_t.shape[1] // 2
    hops = wk.shape[0]
    pairs = graphs // 2
    groups = pairs // 2
    assert nodes == P and feat == 2 * P and hops == 3
    fc = feat // P

    x_d = x.rearrange("(j g) n d -> j n g d", g=2)
    adj_d = adj.rearrange("(j g) n m -> j n g m", g=2)
    adj_t_d = adj_t.rearrange("(j g) m n -> j m g n", g=2)
    out_d = out.rearrange("(j g) n d -> j n g d", g=2)

    with ExitStack() as ctx:
        def sb(name, shape, dt=F32):
            return ctx.enter_context(nc.sbuf_tensor(name, shape, dt))

        def pair_buf(name, shape, dt=F32):
            return [sb(f"{name}_p{p}", shape, dt) for p in range(2)]

        def split_buf(name, shape):
            return [(sb(f"{name}_hi_p{p}", shape, F32R), sb(f"{name}_lo_p{p}", shape, F32R)) for p in range(2)]

        def weight(name, cols):
            return sb(f"{name}_hi", [P, fc, cols], F32R), sb(f"{name}_lo", [P, fc, cols], F32R)

        w_self, w_agg = weight("w_self", feat), weight("w_agg", feat)
        w_qkv = weight("w_qkv", 2 * att + feat)
        w_gcn = [weight(f"w_gcn{i}", feat) for i in range(3)]
        w_hop = [weight(f"w_hop{i}", feat + 2 * (i == hops - 1)) for i in range(hops)]
        ident = sb("ident", [P, P])
        minus_half = sb("minus_half", [P, 2])
        bias_hid = sb("bias_hid", [P, 2, feat])
        bias_gcn = sb("bias_gcn", [P, feat])
        bias_hops = sb("bias_hops", [P, hops, feat])
        bias_diff = sb("bias_diff", [P, feat])
        minus_bias_diff = sb("minus_bias_diff", [P, feat])
        att_bias = sb("att_bias", [P, 4])
        att_stage = sb("att_stage", [P, fc, feat])
        att_rows_w = sb("att_rows_w", [P, 2, feat])
        att_b_row = sb("att_b_row", [P, feat])
        att_cols_w = sb("att_cols_w", [P, fc, 2])

        x0 = pair_buf("x0", [P, 2, feat])
        x1 = pair_buf("x1", [P, 2, feat])
        x2 = pair_buf("x2", [P, 2, feat])
        x3 = pair_buf("x3", [P, 2, feat])
        x2_bias = pair_buf("x2_bias", [P, 2, feat])
        x3_bias = pair_buf("x3_bias", [P, 2, feat])
        floored = pair_buf("floored", [P, 2, feat])
        y = pair_buf("y", [P, 2, feat])
        stats = [pair_buf(f"stats{l}", [P, 2, 6]) for l in range(4)]
        mean_var = [pair_buf(f"mean_var{l}", [P, 2, 2]) for l in range(4)]
        var_eps = [pair_buf(f"var_eps{l}", [P, 2]) for l in range(4)]
        rstd = [pair_buf(f"rstd{l}", [P, 2]) for l in range(4)]
        minus_mean = {l: pair_buf(f"minus_mean{l}", [P, 2]) for l in SCALED_BY_SCALAR}
        shift = {l: pair_buf(f"shift{l}", [P, 2]) for l in SCALED_BY_SCALAR}
        z = [pair_buf(f"z{l}", [P, 2, feat]) for l in range(4)]
        hT_a = split_buf("hT_a", [P, 2, fc, P])
        hT_c = split_buf("hT_c", [P, 2, fc, P])
        adj_a = pair_buf("adj_a", [P, 2, P])
        adj_c = pair_buf("adj_c", [P, 2, P])
        adjT_a = pair_buf("adjT_a", [P, 2, P])
        adjT_b = pair_buf("adjT_b", [P, 2, P])
        deg = pair_buf("deg", [P, 2])
        deg_floor = pair_buf("deg_floor", [P, 2])
        deg_inv = pair_buf("deg_inv", [P, 2])
        rstd_deg = pair_buf("rstd_deg", [P, 2])
        adjT_a_split = split_buf("adjT_a_split", [P, 2, P])
        sage_y = split_buf("sage_y", [P, 2, feat])
        sage_relu = pair_buf("sage_relu", [P, 2, feat])
        qkv = pair_buf("qkv", [P, 2, 2 * att + feat])
        qk_prod = pair_buf("qk_prod", [P, 2, att])
        logit = pair_buf("logit", [P, 2])
        minus_max = pair_buf("minus_max", [2, 1])
        prob = pair_buf("prob", [2, P])
        prob_sum = pair_buf("prob_sum", [2, 1])
        prob_inv = pair_buf("prob_inv", [2, 1])
        prob_diag = pair_buf("prob_diag", [2, 2])
        prob_col = pair_buf("prob_col", [P, 2])
        nearT = split_buf("nearT", [P, fc, 2, P])
        biased = pair_buf("biased", [P, 2, feat])
        hid = pair_buf("hid", [P, 2, feat])
        att_col = pair_buf("att_col", [P, 2, 2])
        pair_score = pair_buf("pair_score", [P, 2, P])
        leaky = pair_buf("leaky", [P, 2, P])
        expo = pair_buf("expo", [P, 2, P])
        alpha = pair_buf("alpha", [P, 2, P])
        row_sum = pair_buf("row_sum", [P, 2])
        row_inv = pair_buf("row_inv", [P, 2])
        trans = pair_buf("trans", [P, 2, P])
        transT = split_buf("transT", [P, 2, P])
        diff = split_buf("diff", [P, 2, feat])

        stage = [*x2_bias, *z[2], *y, *x3_bias, *z[3]]

        bank = [ctx.enter_context(nc.psum_tensor(f"bank{i}", [P, 512], F32)) for i in range(BANKS)]

        def sem(name):
            return ctx.enter_context(nc.semaphore(name))

        def each(names):
            return {name: sem(name) for name in names.split()}

        mm = {step: sem(f"{step}_mm") for step in TENSOR}
        hi = {s: sem(f"{s}_hi") for s in
              "turn0 sage_y turn1 near1 near2 near3 turn3 diff_y0 diff_y1 trans diff_z".split()}
        read = {s: sem(f"{s}_read") for s in mm}
        got = each("stats0 stats1 stats2 stats3 moments0 moments1 moments2 moments3 var_eps0 var_eps1 var_eps2 "
                   "var_eps3 rstd0 rstd1 rstd2 rstd3 z0 z1 z2 z3 deg deg_floor deg_inv rstd_deg "
                   "adjT_a_hi adjT_a_split x1_0 x1_1 x2 "
                   "minus_max prob prob_inv prob_diag x2_bias x3_bias att_cols "
                   "hid1 hid2 leaky expo alpha row_inv trans y")
        for l in SCALED_BY_SCALAR:
            got |= each(f"minus_mean{l} shift{l}")
        landed = {name: [sem(f"{name}_landed_p{p}") for p in range(2)]
                  for name in "x0 adj_a adjT_a adjT_b adj_c out".split()}
        w_landed = [sem(f"w_landed{i}") for i in range(10)]
        small_landed = sem("small_landed")
        w_hi, w_lo = sem("w_hi"), sem("w_lo")
        const_made = sem("const_made")
        att_made = sem("att_made")
        bias_made = sem("bias_made")

        def active(t, lag):
            return not isinstance(t, int) or 0 <= t - lag < groups

        def run(eng, order, steps):
            def turn(t):
                for step, p, lag in order:
                    if active(t, lag):
                        steps[step](t, (t - lag) * 2 + (p + 1), p)

            last = max(lag for _, _, lag in order)
            for t in range(last + 1):
                turn(t)
            with eng.Fori(last + 1, groups) as t:
                turn(t)
            for t in range(groups, groups + last):
                turn(t)

        def before(n):
            return None if isinstance(n, int) and n <= 2 else n - 2

        def landed_count(n, p):
            return (n + (1 - p)) // 2 * 16 if isinstance(n, int) else (n + (1 - p)) * 8

        block = ctx.enter_context(nc.Block())

        def part(halves, a, b):
            return tuple(h[:, :, a:b] for h in halves)

        w_att = part(w_hop[hops - 1], feat, feat + 2)

        w_sources = [
            (w0_t[feat:2 * feat, :], w_agg), (w0_t[0:feat, :], w_self), (wqk_t, part(w_qkv, 0, 2 * att)),
            (wv_t, part(w_qkv, 2 * att, 2 * att + feat)), (w1, w_gcn[0]), (w2, w_gcn[1]), (w3, w_gcn[2]),
            (wk[2], part(w_hop[2], 0, feat)), (wk[1], w_hop[1]), (wk[0], w_hop[0]),
        ]
        HI_AFTER = {"scale0": (0, 2), "turn0": (2, 4), "turn1": (4, 7), "near1": (7, 10)}
        LO_AFTER = {max("moments0", "degree_inv", key=VECTOR.get): (0, 2), "turn0": (2, 4), "turn1": (4, 7),
                    "near1": (7, 10)}
        W_NEEDED = {"sage_y": 2, "qkv0": 4, "hid1": 7, "diff_y0": 11}
        W_ATT = 11

        def splitting(after, split):
            def with_weights(name, do):
                def both(t, n, p):
                    do(t, n, p)
                    if isinstance(n, int) and n == 1:
                        split(*after[name])
                return both if name in after else do
            return with_weights

        @block.sync
        def _(sp):
            def load(name, dst, src, *readers):
                def do(t, n, p):
                    if before(n) is not None:
                        for reader in readers:
                            sp.wait_ge(reader, before(n))
                    sp.dma_start(dst[p][:], src[n - 1]).then_inc(landed[name][p], 16)
                return do

            def store(t, n, p):
                sp.wait_ge(got["y"], n)
                sp.dma_start(out_d[n - 1], y[p][:]).then_inc(landed["out"][p], 16)

            def weights(i):
                src, (half, _) = w_sources[i]
                cols = half.shape[2]
                sp.dma_start(stage[i][:, :, 0:cols], src.rearrange("(c p) o -> p c o", p=P)).then_inc(w_landed[i], 16)

            def small(dst, src):
                sp.dma_start(dst, src).then_inc(small_landed, 16)

            loads = {
                "x0": load("x0", x0, x_d, got["x1_0"], got["x1_1"]),
                "adj_a": load("adj_a", adj_a, adj_d, got["deg"]),
                "adjT_a": load("adjT_a", adjT_a, adj_t_d, mm["adj_k"]),
                "adjT_b": load("adjT_b", adjT_b, adj_t_d, mm["near3"]),
                "adj_c": load("adj_c", adj_c, adj_d, got["alpha"]),
            }
            loads["x0"](0, 1, 0)
            loads["adj_a"](0, 1, 0)
            weights(0)
            weights(1)
            loads["x0"](0, 2, 1)
            loads["adj_a"](0, 2, 1)
            for name in ("adjT_a", "adjT_b", "adj_c"):
                for p in range(2):
                    loads[name](0, p + 1, p)
            for i in range(2, len(w_sources)):
                weights(i)
            small(bias_hid[:], b12.partition_broadcast(P))
            small(bias_gcn[:], b3.partition_broadcast(P))
            small(bias_hops[:], bk.partition_broadcast(P))
            small(att_stage[:], att_w.rearrange("(c p) o -> p c o", p=P))
            small(att_rows_w[:], att_vec.rearrange("(s d) o -> (o s) d", s=2).partition_broadcast(P))
            small(att_b_row[:], att_b.partition_broadcast(P))
            small(att_bias[:, 0:1], att_c.partition_broadcast(P))

            def next_load(do):
                def later(t, n, p):
                    if not isinstance(n, int) or n > 2:
                        do(t, n, p)
                return later

            run(sp, in_order(SYNC), {"store": store} | {name: next_load(do) for name, do in loads.items()})
            for p in range(2):
                sp.wait_ge(landed["out"][p], 16 * groups)

        @block.gpsimd
        def _(pool):
            nc.gpsimd.memset(ident[:], 0.0).then_inc(const_made, 1)
            pool.wait_ge(const_made, 1)
            nc.gpsimd.affine_select(out=ident[:], in_=ident[:], compare_op=ALU.not_equal, fill=1.0, base=0,
                                    pattern=[[-1, P]], channel_multiplier=1).then_inc(const_made, 1)
            nc.gpsimd.memset(minus_half[:], -0.5).then_inc(const_made, 1)
            pool.wait_ge(const_made, 3)

            def inverse_deviation(l):
                def do(t, n, p):
                    pool.wait_ge(got[f"moments{l}"], n)
                    pool.nop(nofuse=True)
                    nc.gpsimd.tensor_scalar(var_eps[l][p][:], mean_var[l][p][:, :, 1], LAYERNORM_EPS, None,
                                            ALU.add).then_inc(got[f"var_eps{l}"], 1)
                    if l in SCALED_BY_SCALAR:
                        nc.gpsimd.tensor_scalar(minus_mean[l][p][:], mean_var[l][p][:, :, 0], -1.0, None,
                                                ALU.mult).then_inc(got[f"minus_mean{l}"], 1)
                    pool.wait_ge(got[f"var_eps{l}"], n)
                    nc.gpsimd.tensor_tensor(rstd[l][p][:], var_eps[l][p][:], minus_half[:],
                                            ALU.pow).then_inc(got[f"rstd{l}"], 1)
                    if l not in SCALED_BY_SCALAR:
                        return
                    pool.wait_ge(got[f"rstd{l}"], n)
                    factor = rstd[l][p]
                    if l == 0:
                        pool.wait_ge(got["deg_floor"], n)
                        factor = rstd_deg[p]
                        nc.gpsimd.tensor_tensor(factor[:], rstd[l][p][:], deg_floor[p][:],
                                                ALU.mult).then_inc(got["rstd_deg"], 1)
                        pool.wait_ge(got["rstd_deg"], n)
                    pool.wait_ge(got[f"minus_mean{l}"], n)
                    nc.gpsimd.tensor_tensor(shift[l][p][:], minus_mean[l][p][:], factor[:],
                                            ALU.mult).then_inc(got[f"shift{l}"], 1)
                return do

            def adj_lo(t, n, p):
                pool.wait_ge(got["adjT_a_hi"], n)
                h, l = adjT_a_split[p]
                nc.gpsimd.tensor_tensor(l[:], adjT_a[p][:], h[:].bitcast(F32),
                                        ALU.subtract).then_inc(got["adjT_a_split"], 1)

            def x2_plus_bias(t, n, p):
                pool.wait_ge(got["x2"], n)
                if before(n) is not None:
                    pool.wait_ge(read["gcn0"], before(n))
                    pool.wait_ge(read["gcn1"], before(n))
                if isinstance(n, int) and n == 1:
                    pool.wait_ge(small_landed, 16 * SMALL_LOADS)
                nc.gpsimd.tensor_tensor(x2_bias[p][:], x2[p][:], bias_gcn[:].unsqueeze(1).to_broadcast([P, 2, feat]),
                                        ALU.add).then_inc(got["x2_bias"], 1)

            def x3_plus_bias(t, n, p):
                pool.wait_ge(read["gcn0"], n)
                pool.wait_ge(read["gcn1"], n)
                if isinstance(n, int) and n == 1:
                    pool.wait_ge(bias_made, hops)
                if before(n) is not None:
                    pool.wait_ge(got["y"], before(n))
                nc.gpsimd.tensor_tensor(x3_bias[p][:], x3[p][:], bias_diff[:].unsqueeze(1).to_broadcast([P, 2, feat]),
                                        ALU.add).then_inc(got["x3_bias"], 1)

            def finish(t, n, p):
                pool.wait_ge(got["x3_bias"], n)
                if before(n) is not None:
                    pool.wait_ge(landed["out"][p], landed_count(n, p) - 16)
                pool.wait_ge(read["diffuse"], n)
                nc.gpsimd.tensor_tensor(y[p][:], floored[p][:], x3_bias[p][:], ALU.add).then_inc(got["y"], 1)

            run(pool, in_order(GPSIMD), {
                "rstd0": inverse_deviation(0), "rstd1": inverse_deviation(1), "rstd2": inverse_deviation(2),
                "rstd3": inverse_deviation(3), "adj_lo": adj_lo, "x2_bias": x2_plus_bias, 
                "x3_bias": x3_plus_bias, "y": finish,
            })

        tensor_order = in_order(TENSOR)
        bank_of = {(step, p): bank[i % BANKS] for i, (step, p, _) in enumerate(tensor_order)}
        assert len(tensor_order) % BANKS == 0

        def view(step, p, *dims):
            size = 1
            for d in dims:
                size *= d
            b = bank_of[step, p][:, 0:size]
            if len(dims) == 2:
                return b.rearrange("p (a b) -> p a b", b=dims[1])
            if len(dims) == 3:
                return b.rearrange("p (a b c) -> p a b c", b=dims[1], c=dims[2])
            return b

        @block.scalar
        def _(act):
            def weights(first, end):
                for i in range(first, end):
                    half = w_sources[i][1][0]
                    act.wait_ge(w_landed[i], 16)
                    nc.scalar.activation(half[:, :, :], stage[i][:, :, 0:half.shape[2]], ACT.Copy).then_inc(w_hi, 1)

            def attention_hi(t, n, p):
                take_hi("turn3", hT_c, ACT.Relu, 2, fc, P)(t, n, p)
                if isinstance(n, int) and n == 1:
                    act.wait_ge(att_made, 2 * fc)
                    nc.scalar.activation(w_att[0], att_cols_w[:], ACT.Copy).then_inc(w_hi, 1)

            def take_hi(step, halves, func, *dims):
                def do(t, n, p):
                    act.wait_ge(mm[step], n)
                    nc.scalar.activation(halves[p][0][:], view(step, p, *dims), func).then_inc(hi[step], 1)
                return do

            def scale(l, src):
                func, user = (ACT.Relu, "near1") if l == 2 else (ACT.Identity, f"turn{l}")

                def do(t, n, p):
                    act.wait_ge(got[f"shift{l}"], n)
                    if before(n) is not None:
                        act.wait_ge(mm[user], before(n))
                    factor = rstd_deg[p] if l == 0 else rstd[l][p]
                    for g in range(2):
                        last = nc.scalar.activation(z[l][p][:, g, :], src[p][:, g, :], func,
                                                    bias=shift[l][p][:, g:g + 1], scale=factor[:, g:g + 1])
                    last.then_inc(got[f"z{l}"], 1)
                return do

            def adj_hi(t, n, p):
                act.wait_ge(landed["adjT_a"][p], landed_count(n, p))
                if before(n) is not None:
                    for g in range(2):
                        act.wait_ge(mm[f"sage{g}"], before(n))
                nc.scalar.activation(adjT_a_split[p][0][:], adjT_a[p][:], ACT.Copy).then_inc(got["adjT_a_hi"], 1)

            def sage_y_hi(t, n, p):
                act.wait_ge(mm["sage_y"], n)
                act.wait_ge(got["deg_inv"], n)
                v = view("sage_y", p, 2, feat)
                for g in range(2):
                    last = nc.scalar.activation(sage_y[p][0][:, g, :], v[:, g, :], ACT.Copy,
                                                scale=deg_inv[p][:, g:g + 1])
                last.then_inc(hi["sage_y"], 1)

            def sage(step, g):
                def do(t, n, p):
                    act.wait_ge(mm[step], n)
                    if before(n) is not None:
                        act.wait_ge(got[f"x1_{g}"], before(n))
                    nc.scalar.activation(sage_relu[p][:, g, :], view(step, p, feat), ACT.Relu,
                                         scale=deg_inv[p][:, g:g + 1]).then_inc(read[step], 1)
                return do

            def transition(t, n, p):
                act.wait_ge(got["row_inv"], n)
                if before(n) is not None:
                    act.wait_ge(mm["trans"], before(n))
                for g in range(2):
                    last = nc.scalar.activation(trans[p][:, g, :], alpha[p][:, g, :], ACT.Copy,
                                                scale=row_inv[p][:, g:g + 1])
                last.then_inc(got["trans"], 1)

            def take_qkv(step, g):
                def do(t, n, p):
                    act.wait_ge(mm[step], n)
                    if before(n) is not None:
                        act.wait_ge(got["x2"], before(n))
                    nc.scalar.activation(qkv[p][:, g, :], view(step, p, 2 * att + feat),
                                         ACT.Copy).then_inc(read[step], 1)
                return do

            def take_hi_graph(step, g):
                def do(t, n, p):
                    act.wait_ge(mm[step], n)
                    nc.scalar.activation(diff[p][0][:, g, :], view(step, p, feat), ACT.Copy).then_inc(hi[step], 1)
                return do

            def softmax(t, n, p):
                act.wait_ge(got["minus_max"], n)
                if before(n) is not None:
                    act.wait_ge(mm["prob_col"], before(n))
                nc.scalar.activation(prob[p][:], view("logit_row", p, P)[0:2, :], ACT.Exp, bias=minus_max[p][:, 0:1],
                                     accum_out=prob_sum[p][:, 0:1]).then_inc(got["prob"], 1)

            def hidden(step):
                def do(t, n, p):
                    act.wait_ge(read[step], n)
                    if step == "hid1" and before(n) is not None:
                        act.wait_ge(mm["near3"], before(n))
                    nc.scalar.activation(hid[p][:], biased[p][:], ACT.Relu).then_inc(got[step], 1)
                return do

            def att_rows(t, n, p):
                act.wait_ge(mm["att_rows"], n)
                v = view("att_rows", p, 2, P)
                if before(n) is not None:
                    act.wait_ge(got["leaky"], before(n))
                for g in range(2):
                    last = nc.scalar.activation(pair_score[p][:, g, :], v[:, g, :], ACT.Identity,
                                                bias=att_col[p][:, g, 1:2])
                last.then_inc(read["att_rows"], 1)

            def exponent(t, n, p):
                act.wait_ge(got["leaky"], n)
                if before(n) is not None:
                    act.wait_ge(got["alpha"], before(n))
                nc.scalar.activation(expo[p][:], leaky[p][:], ACT.Exp).then_inc(got["expo"], 1)

            steps = {f"scale{l}": scale(l, src) for l, src in enumerate((x0, x1, x2, x3)) if l in SCALED_BY_SCALAR} | {
                "adj_hi": adj_hi, "sage0": sage("sage0", 0), "sage1": sage("sage1", 1),
                "turn0": take_hi("turn0", hT_a, ACT.Relu, 2, fc, P),
                "sage_y": sage_y_hi,
                "turn1": take_hi("turn1", hT_a, ACT.Relu, 2, fc, P),
                "qkv0": take_qkv("qkv0", 0), "qkv1": take_qkv("qkv1", 1), "softmax": softmax,
                "near1": take_hi("near1", nearT, ACT.Copy, fc, 2, P), "hid1": hidden("hid1"),
                "near2": take_hi("near2", nearT, ACT.Copy, fc, 2, P), "hid2": hidden("hid2"),
                "near3": take_hi("near3", nearT, ACT.Copy, fc, 2, P),
                "turn3": attention_hi,
                "diff_y0": take_hi_graph("diff_y0", 0), "diff_y1": take_hi_graph("diff_y1", 1),
                "att_rows": att_rows, "exponent": exponent, "transition": transition,
                "trans": take_hi("trans", transT, ACT.Copy, 2, P),
                "diff_z": take_hi("diff_z", diff, ACT.Copy, 2, feat),
            }
            with_weights = splitting(HI_AFTER, weights)
            run(act, in_order(SCALAR), {name: with_weights(name, do) for name, do in steps.items()})

        @block.vector
        def _(dve):
            def weights(first, end):
                for i in range(first, end):
                    h, l = w_sources[i][1]
                    dve.wait_ge(w_hi, i + 1)
                    nc.vector.tensor_tensor(l[:, :, :], stage[i][:, :, 0:h.shape[2]], h[:, :, :].bitcast(F32),
                                            ALU.subtract).then_inc(w_lo, 1)

            def diffusion_bias():
                for i in range(1, hops):
                    other = bias_hops[:, 0, :] if i == 1 else bias_diff[:]
                    if i > 1:
                        dve.wait_ge(bias_made, i - 1)
                    nc.vector.tensor_tensor(bias_diff[:], other, bias_hops[:, i, :], ALU.add).then_inc(bias_made, 1)
                dve.wait_ge(bias_made, hops - 1)
                nc.vector.tensor_scalar(minus_bias_diff[:], bias_diff[:], -1.0, None, ALU.mult).then_inc(bias_made, 1)

            def attention_weights():
                junk = leaky[0][:].rearrange("p g m -> p (g m)")
                for c in range(fc):
                    for s in range(2):
                        nc.vector.tensor_tensor_reduce(junk, att_stage[:, c, :], att_rows_w[:, s, :], 1.0,
                                                       0.0, ALU.mult, ALU.add,
                                                       att_cols_w[:, c, s:s + 1]).then_inc(att_made, 1)
                        dve.wait_ge(att_made, fc * c + s + 1)
                for s in range(2):
                    nc.vector.tensor_tensor_reduce(junk, att_b_row[:], att_rows_w[:, s, :], 1.0, 0.0,
                                                   ALU.mult, ALU.add, att_bias[:, s + 1:s + 2]).then_inc(att_made, 1)
                    dve.wait_ge(att_made, 2 * fc + s + 1)
                nc.vector.reduce_sum(att_bias[:, 3:4], att_bias[:, 0:3], AX_X).then_inc(att_made, 1)

            def near3(t, n, p):
                take_lo("near3", nearT, fc, 2, P)(t, n, p)
                if isinstance(n, int) and n == 1:
                    diffusion_bias()
                    attention_weights()

            def turn3(t, n, p):
                take_relu_lo("turn3", hT_c)(t, n, p)
                if isinstance(n, int) and n == 1:
                    dve.wait_ge(w_hi, W_ATT)
                    nc.vector.tensor_tensor(w_att[1], att_cols_w[:], w_att[0].bitcast(F32),
                                            ALU.subtract).then_inc(w_lo, 1)

            def layer_stats(l, src, ready):
                def do(t, n, p):
                    if l == 0:
                        dve.wait_ge(landed["x0"][p], landed_count(n, p))
                    for r in ready:
                        dve.wait_ge(r, n)
                    for g in range(2):
                        last = nc.vector.bn_stats(stats[l][p][:, g, :], src[p][:, g, :])
                    last.then_inc(got[f"stats{l}"], 1)
                return do

            def moments(l):
                def do(t, n, p):
                    dve.wait_ge(got[f"stats{l}"], n)
                    dve.nop(nofuse=True)
                    if before(n) is not None:
                        dve.wait_ge(got[f"z{l}"], before(n))
                        dve.nop(nofuse=True)
                    for g in range(2):
                        last = nc.vector.bn_aggr(mean_var[l][p][:, g, :], stats[l][p][:, g, :])
                    last.then_inc(got[f"moments{l}"], 1)
                return do

            def scale(l, src):
                def do(t, n, p):
                    dve.wait_ge(got[f"rstd{l}"], n)
                    if before(n) is not None:
                        dve.wait_ge(mm[f"turn{l}"], before(n))
                    for g in range(2):
                        last = nc.vector.tensor_scalar(z[l][p][:, g, :], src[p][:, g, :], mean_var[l][p][:, g, 0:1],
                                                       rstd[l][p][:, g:g + 1], ALU.subtract, ALU.mult)
                    last.then_inc(got[f"z{l}"], 1)
                return do

            def degree(t, n, p):
                dve.wait_ge(landed["adj_a"][p], landed_count(n, p))
                nc.vector.reduce_sum(deg[p][:], adj_a[p][:], AX_X).then_inc(got["deg"], 1)

            def degree_inverse(t, n, p):
                dve.wait_ge(got["deg"], n)
                if before(n) is not None:
                    dve.wait_ge(got["rstd_deg"], before(n))
                nc.vector.tensor_scalar(deg_floor[p][:], deg[p][:], DEGREE_EPS, None,
                                        ALU.max).then_inc(got["deg_floor"], 1)
                dve.wait_ge(got["deg_floor"], n)
                if before(n) is not None:
                    for g in range(2):
                        dve.wait_ge(read[f"sage{g}"], before(n))
                nc.vector.reciprocal(deg_inv[p][:], deg_floor[p][:]).then_inc(got["deg_inv"], 1)

            def take_lo(step, halves, *dims):
                def do(t, n, p):
                    h, l = halves[p]
                    dve.wait_ge(hi[step], n)
                    nc.vector.tensor_tensor(l[:], view(step, p, *dims), h[:].bitcast(F32),
                                            ALU.subtract).then_inc(read[step], 1)
                return do

            def take_relu_lo(step, halves):
                def do(t, n, p):
                    h, l = halves[p]
                    dve.wait_ge(hi[step], n)
                    b = bank_of[step, p][:]
                    nc.vector.scalar_tensor_tensor(l[:].rearrange("p a b c -> p (a b c)"), b, 0.0,
                                                   h[:].bitcast(F32).rearrange("p a b c -> p (a b c)"), ALU.max,
                                                   ALU.subtract).then_inc(read[step], 1)
                return do

            def sage_y_lo(t, n, p):
                dve.wait_ge(hi["sage_y"], n)
                h, l = sage_y[p]
                v = view("sage_y", p, 2, feat)
                for g in range(2):
                    last = nc.vector.scalar_tensor_tensor(l[:, g, :], v[:, g, :], deg_inv[p][:, g:g + 1],
                                                          h[:, g, :].bitcast(F32), ALU.mult, ALU.subtract)
                last.then_inc(read["sage_y"], 1)

            def sage(step, g):
                def do(t, n, p):
                    dve.wait_ge(read[step], n)
                    nc.vector.tensor_tensor(x1[p][:, g, :], sage_relu[p][:, g, :], x0[p][:, g, :],
                                            ALU.add).then_inc(got[f"x1_{g}"], 1)
                return do

            def adj_k(t, n, p):
                dve.wait_ge(mm["adj_k"], n)
                if before(n) is not None:
                    dve.wait_ge(mm["logit_row"], before(n))
                v = view("adj_k", p, 2, att)
                for g in range(2):
                    last = nc.vector.tensor_tensor_reduce(qk_prod[p][:, g, :], v[:, g, :], qkv[p][:, g, 0:att],
                                                          float(att) ** -0.5, 0.0,
                                                          ALU.mult, ALU.add, logit[p][:, g:g + 1])
                last.then_inc(read["adj_k"], 1)

            def logit_row(t, n, p):
                dve.wait_ge(mm["logit_row"], n)
                if before(n) is not None:
                    dve.wait_ge(got["prob"], before(n))
                nc.vector.reduce_max(minus_max[p][:], view("logit_row", p, P)[0:2, :], AX_X,
                                     negate=True).then_inc(got["minus_max"], 1)

            def quotient(t, n, p):
                dve.wait_ge(got["prob"], n)
                nc.vector.reciprocal(prob_inv[p][:], prob_sum[p][:]).then_inc(got["prob_inv"], 1)
                dve.wait_ge(got["prob_inv"], n)
                if isinstance(n, int) and n == 1:
                    dve.wait_ge(const_made, 3)
                if before(n) is not None:
                    dve.wait_ge(mm["prob_col"], before(n))
                nc.vector.tensor_scalar(prob_diag[p][:], ident[0:2, 0:2], prob_inv[p][:, 0:1], None,
                                        ALU.mult).then_inc(got["prob_diag"], 1)

            def prob_column(t, n, p):
                dve.wait_ge(mm["prob_col"], n)
                nc.vector.tensor_copy(prob_col[p][:], view("prob_col", p, 2)).then_inc(read["prob_col"], 1)

            def attend(t, n, p):
                dve.wait_ge(read["prob_col"], n)
                if before(n) is not None:
                    dve.wait_ge(got["x2_bias"], before(n))
                for g in range(2):
                    last = nc.vector.scalar_tensor_tensor(x2[p][:, g, :], qkv[p][:, g, 2 * att:],
                                                          prob_col[p][:, g:g + 1], x1[p][:, g, :], ALU.mult, ALU.add)
                last.then_inc(got["x2"], 1)

            def hidden(step, layer):
                def do(t, n, p):
                    dve.wait_ge(mm[step], n)
                    if step == "hid2":
                        dve.wait_ge(got["hid1"], n)
                    elif before(n) is not None:
                        dve.wait_ge(got["hid2"], before(n))
                    if isinstance(n, int) and n == 1:
                        dve.wait_ge(small_landed, 16 * SMALL_LOADS)
                    nc.vector.tensor_tensor(biased[p][:], view(step, p, 2, feat),
                                            bias_hid[:, layer, :].unsqueeze(1).to_broadcast([P, 2, feat]),
                                            ALU.add).then_inc(read[step], 1)
                return do

            def gcn(step, g):
                def do(t, n, p):
                    dve.wait_ge(mm[step], n)
                    dve.wait_ge(got["x2_bias"], n)
                    if before(n) is not None:
                        dve.wait_ge(got["x3_bias"], before(n))
                    nc.vector.tensor_tensor(x3[p][:, g, :], view(step, p, feat), x2_bias[p][:, g, :],
                                            ALU.add).then_inc(read[step], 1)
                return do

            def diff_y(step, g):
                def do(t, n, p):
                    dve.wait_ge(hi[step], n)
                    v = view(step, p, feat + 2)
                    if before(n) is not None:
                        dve.wait_ge(read["att_rows"], before(n))
                    nc.vector.tensor_copy(att_col[p][:, g, 0:1], v[:, feat:feat + 1])
                    last = nc.vector.tensor_scalar(att_col[p][:, g, 1:2], v[:, feat + 1:feat + 2], att_bias[:, 3:4],
                                                   None, ALU.add)
                    if g == 1:
                        last.then_inc(got["att_cols"], 1)
                    h, l = diff[p]
                    nc.vector.tensor_tensor(l[:, g, :], v[:, 0:feat], h[:, g, :].bitcast(F32),
                                            ALU.subtract).then_inc(read[step], 1)
                return do

            def leaky_relu(t, n, p):
                dve.wait_ge(read["att_rows"], n)
                if before(n) is not None:
                    dve.wait_ge(got["expo"], before(n))
                s = pair_score[p][:]
                nc.vector.scalar_tensor_tensor(leaky[p][:], s, LEAKY_SLOPE, s, ALU.mult,
                                               ALU.max).then_inc(got["leaky"], 1)

            def alpha_rows(t, n, p):
                dve.wait_ge(landed["adj_c"][p], landed_count(n, p))
                if before(n) is not None:
                    dve.wait_ge(got["trans"], before(n))
                dve.wait_ge(got["expo"], n)
                for g in range(2):
                    last = nc.vector.tensor_tensor_reduce(alpha[p][:, g, :], adj_c[p][:, g, :], expo[p][:, g, :], 1.0,
                                                          ROW_SUM_EPS, ALU.mult, ALU.add, row_sum[p][:, g:g + 1])
                last.then_inc(got["alpha"], 1)

            def row_inverse(t, n, p):
                dve.wait_ge(got["alpha"], n)
                nc.vector.reciprocal(row_inv[p][:], row_sum[p][:]).then_inc(got["row_inv"], 1)

            def diffuse(t, n, p):
                dve.wait_ge(mm["diffuse"], n)
                if before(n) is not None:
                    dve.wait_ge(got["y"], before(n))
                nc.vector.tensor_tensor(floored[p][:], view("diffuse", p, 2, feat),
                                        minus_bias_diff[:].unsqueeze(1).to_broadcast([P, 2, feat]),
                                        ALU.max).then_inc(read["diffuse"], 1)

            steps = {
                "stats0": layer_stats(0, x0, []), "stats1": layer_stats(1, x1, [got["x1_0"], got["x1_1"]]),
                "stats2": layer_stats(2, x2, [got["x2"]]), "stats3": layer_stats(3, x3, [read["gcn0"], read["gcn1"]]),
                "moments0": moments(0), "moments1": moments(1), "moments2": moments(2), "moments3": moments(3),
                "degree": degree, "degree_inv": degree_inverse,
                "turn0": take_relu_lo("turn0", hT_a), "turn1": take_relu_lo("turn1", hT_a),
                "turn3": turn3,
                "sage_y": sage_y_lo, "sage0": sage("sage0", 0), "sage1": sage("sage1", 1), "adj_k": adj_k,
                "logit_row": logit_row, "quotient": quotient, "prob_col": prob_column, "attend": attend,
                "near1": take_lo("near1", nearT, fc, 2, P),
                "hid1": hidden("hid1", 0), "near2": take_lo("near2", nearT, fc, 2, P), "hid2": hidden("hid2", 1),
                "near3": near3, "gcn0": gcn("gcn0", 0), "gcn1": gcn("gcn1", 1),
                "diff_y0": diff_y("diff_y0", 0), "diff_y1": diff_y("diff_y1", 1),
                "leaky": leaky_relu, "alpha": alpha_rows, "row_inv": row_inverse,
                "trans": take_lo("trans", transT, 2, P), "diff_z": take_lo("diff_z", diff, 2, feat),
                "diffuse": diffuse,
            }
            steps |= {f"scale{l}": scale(l, src) for l, src in enumerate((x0, x1, x2, x3)) if l not in SCALED_BY_SCALAR}
            with_weights = splitting(LO_AFTER, weights)
            run(dve, in_order(VECTOR), {name: with_weights(name, do) for name, do in steps.items()})

        @block.tensor
        def _(pe):
            place_of = {(step, p): i for i, (step, p, _) in enumerate(tensor_order)}

            def free_bank(t, step, p):
                at, back = place_of[step, p], 0
                while True:
                    at -= BANKS
                    if at < 0:
                        at, back = at + len(tensor_order), back + 1
                    user, q, lag = tensor_order[at]
                    if isinstance(t, int) and t < back:
                        return
                    if active(t - back if isinstance(t, int) else t, lag):
                        break
                user_read = got["prob"] if user == "logit_row" else read[user]
                pe.wait_ge(user_read, (t - back - lag) * 2 + (q + 1))

            def product(out_ap, left, right, start=True, stop=True):
                (lh, ll), (rh, rl) = left, right
                nc.tensor.matmul(out_ap, lh, rl, start=start, stop=False, skip_group_check=True)
                nc.tensor.matmul(out_ap, ll, rh, start=False, stop=False, skip_group_check=True)
                return nc.tensor.matmul(out_ap, lh, rh, start=False, stop=stop, skip_group_check=True)

            def pick(halves, *index):
                return tuple(h[(slice(None), *index)] for h in halves)

            def turn(step, l):
                def do(t, n, p):
                    free_bank(t, step, p)
                    pe.wait_ge(got[f"z{l}"], n)
                    v = view(step, p, 2, fc, P)
                    for g in range(2):
                        for c in range(fc):
                            last = nc.tensor.transpose(v[:, g, c, :], z[l][p][:, g, c * P:(c + 1) * P], ident[:])
                    last.then_inc(mm[step], 1)
                return do

            def turn_rows(step, src, ready):
                def do(t, n, p):
                    free_bank(t, step, p)
                    pe.wait_ge(got[ready], n)
                    v = view(step, p, 2, P)
                    for g in range(2):
                        last = nc.tensor.transpose(v[:, g, :], src[p][:, g, :], ident[:])
                    last.then_inc(mm[step], 1)
                return do

            def first_use(step, n):
                if isinstance(n, int) and n == 1 and step in W_NEEDED:
                    pe.wait_ge(w_lo, W_NEEDED[step])

            def project(step, actT, ready, w, cols):
                def do(t, n, p):
                    free_bank(t, step, p)
                    first_use(step, n)
                    pe.wait_ge(ready, n)
                    v = view(step, p, 2, cols)
                    for g in range(2):
                        for c in range(fc):
                            last = product(v[:, g, :], pick(actT[p], g, c), pick(w, c), start=c == 0,
                                           stop=c == fc - 1)
                    last.then_inc(mm[step], 1)
                return do

            def project_graph(step, g, actT, ready, w, cols):
                def do(t, n, p):
                    free_bank(t, step, p)
                    first_use(step, n)
                    pe.wait_ge(ready, n)
                    for c in range(fc):
                        last = product(view(step, p, cols), pick(actT[p], g, c), pick(w, c), start=c == 0,
                                       stop=c == fc - 1)
                    last.then_inc(mm[step], 1)
                return do

            def project_near(step, layer):
                def do(t, n, p):
                    free_bank(t, step, p)
                    first_use(step, n)
                    pe.wait_ge(read[f"near{layer + 1}"], n)
                    v = view(step, p, 2, feat)
                    for g in range(2):
                        for c in range(fc):
                            last = product(v[:, g, :], pick(nearT[p], c, g), pick(w_gcn[layer], c), start=c == 0,
                                           stop=c == fc - 1)
                    last.then_inc(mm[step], 1)
                return do

            def project_last(step, g):
                def do(t, n, p):
                    free_bank(t, step, p)
                    pe.wait_ge(read["near3"], n)
                    for c in range(fc):
                        last = product(view(step, p, feat), pick(nearT[p], c, g), pick(w_gcn[2], c), start=c == 0,
                                       stop=c == fc - 1)
                    last.then_inc(mm[step], 1)
                return do

            def project_and_spread(step, actT, ready, w, nodesT, moved, moved_ready):
                def do(t, n, p):
                    free_bank(t, step, p)
                    pe.wait_ge(ready, n)
                    v = view(step, p, 2, feat)
                    for g in range(2):
                        for c in range(fc):
                            product(v[:, g, :], pick(actT[p], g, c), pick(w, c), start=g == 0 and c == 0, stop=False)
                    for r in moved_ready:
                        pe.wait_ge(r, n)
                    for g in range(2):
                        last = product(v[:, g, :], pick(nodesT[p], g), pick(moved[p], g), start=False, stop=True)
                    last.then_inc(mm[step], 1)
                return do

            def sage(step, g):
                def do(t, n, p):
                    free_bank(t, step, p)
                    first_use(step, n)
                    pe.wait_ge(read["turn0"], n)
                    v = view(step, p, feat)
                    for c in range(fc):
                        product(v, pick(hT_a[p], g, c), pick(w_self, c), start=c == 0, stop=False)
                    pe.wait_ge(got["adjT_a_split"], n)
                    pe.wait_ge(read["sage_y"], n)
                    product(v, pick(adjT_a_split[p], g), pick(sage_y[p], g), start=False).then_inc(mm[step], 1)
                return do

            def spread(step, h, ready):
                def do(t, n, p):
                    free_bank(t, step, p)
                    pe.wait_ge(ready, n)
                    if step == "near1":
                        pe.wait_ge(landed["adjT_b"][p], landed_count(n, p))
                    v = view(step, p, fc, 2, P)
                    for g in range(2):
                        for c in range(fc):
                            last = nc.tensor.matmul(v[:, c, g, :], h[p][:, g, c * P:(c + 1) * P], adjT_b[p][:, g, :],
                                                    start=True, stop=True)
                    last.then_inc(mm[step], 1)
                return do

            def adj_k(t, n, p):
                free_bank(t, "adj_k", p)
                pe.wait_ge(read["qkv0"], n)
                pe.wait_ge(read["qkv1"], n)
                pe.wait_ge(landed["adjT_a"][p], landed_count(n, p))
                v = view("adj_k", p, 2, att)
                for g in range(2):
                    last = nc.tensor.matmul(v[:, g, :], adjT_a[p][:, g, :], qkv[p][:, g, att:2 * att], start=True,
                                            stop=True)
                last.then_inc(mm["adj_k"], 1)

            def logit_row(t, n, p):
                free_bank(t, "logit_row", p)
                pe.wait_ge(read["adj_k"], n)
                nc.tensor.matmul(view("logit_row", p, P)[0:2, :], logit[p][:], ident[:], start=True,
                                 stop=True).then_inc(mm["logit_row"], 1)

            def prob_column(t, n, p):
                free_bank(t, "prob_col", p)
                pe.wait_ge(got["prob_diag"], n)
                nc.tensor.matmul(view("prob_col", p, 2), prob[p][:], prob_diag[p][:], start=True,
                                 stop=True).then_inc(mm["prob_col"], 1)

            def att_rows(t, n, p):
                free_bank(t, "att_rows", p)
                pe.wait_ge(got["att_cols"], n)
                v = view("att_rows", p, 2, P)
                for g in range(2):
                    last = nc.tensor.transpose(v[:, g, :], att_col[p][:, g, 0:1].to_broadcast([P, P]), ident[:])
                last.then_inc(mm["att_rows"], 1)

            pe.wait_ge(const_made, 3)
            run(pe, tensor_order, {
                "turn0": turn("turn0", 0),
                "sage_y": project("sage_y", hT_a, read["turn0"], w_agg, feat),
                "sage0": sage("sage0", 0), "sage1": sage("sage1", 1),
                "turn1": turn("turn1", 1),
                "qkv0": project_graph("qkv0", 0, hT_a, read["turn1"], w_qkv, 2 * att + feat),
                "qkv1": project_graph("qkv1", 1, hT_a, read["turn1"], w_qkv, 2 * att + feat),
                "adj_k": adj_k,
                "logit_row": logit_row,
                "prob_col": prob_column,
                "near1": spread("near1", z[2], got["z2"]), "hid1": project_near("hid1", 0),
                "near2": spread("near2", hid, got["hid1"]), "hid2": project_near("hid2", 1),
                "near3": spread("near3", hid, got["hid2"]),
                "gcn0": project_last("gcn0", 0), "gcn1": project_last("gcn1", 1),
                "turn3": turn("turn3", 3),
                "diff_y0": project_graph("diff_y0", 0, hT_c, read["turn3"], w_hop[2], feat + 2),
                "diff_y1": project_graph("diff_y1", 1, hT_c, read["turn3"], w_hop[2], feat + 2),
                "att_rows": att_rows,
                "trans": turn_rows("trans", trans, "trans"),
                "diff_z": project_and_spread("diff_z", hT_c, read["turn3"], w_hop[1], transT, diff,
                                             [read["trans"], read["diff_y0"], read["diff_y1"]]),
                "diffuse": project_and_spread("diffuse", hT_c, read["turn3"], w_hop[0], transT, diff,
                                              [read["diff_z"]]),
            })


_OUT = (128, 128, 256)


def kernel(**inputs):
    import numpy as _np
    import concourse.bacc as _bacc
    from concourse import mybir as _mybir
    from concourse.bass_utils import run_bass_kernel_spmd as _run

    given = {name: _np.asarray(a) for name, a in inputs.items()}
    laid_out = [
        ("x", given["x"]), ("adj", given["adj"]), ("adj_t", given["adj"].transpose(0, 2, 1)),
        ("w0_t", given["L0_gnn_W"].T), ("wqk_t", given["L1_gnn_W_qk"].T), ("wv_t", given["L1_gnn_W_v"].T),
        ("w1", given["L2_gnn_W1"]), ("w2", given["L2_gnn_W2"]), ("w3", given["L2_gnn_W3"]),
        ("b12", _np.stack([given["L2_gnn_b1"], given["L2_gnn_b2"]])),
        ("b3", given["L2_gnn_b3"]),
        ("att_w", given["L3_gnn_Wv"]), ("att_b", given["L3_gnn_bv"]), ("att_vec", given["L3_gnn_aw"]),
        ("att_c", given["L3_gnn_ab"]), ("wk", given["L3_gnn_Wk"]), ("bk", given["L3_gnn_bk"]),
    ]
    nc = _bacc.Bacc("TRN2", target_bir_lowering=False, num_devices=1)
    arrays, args = {}, []
    for name, a in laid_out:
        a = _np.ascontiguousarray(a)
        arrays[f"in_{name}_dram"] = a
        args.append(nc.dram_tensor(f"in_{name}_dram", a.shape, _mybir.dt.from_np(a.dtype), kind="ExternalInput").ap())
    args.append(nc.dram_tensor("out_dram", _OUT, _mybir.dt.float32, kind="ExternalOutput").ap())
    build(nc, *args)
    r = _run(nc, [arrays], core_ids=[0])
    return r.results[0]["out_dram"]
```
